# Optimizing a Trainium2 kernel written in Bass

```python
import numpy as np
import jax
import jax.numpy as jnp

def _softmax(x, axis=-1):
    return jax.nn.softmax(x, axis=axis)

def _gelu(x):
    return jax.nn.gelu(x, approximate=True)

def _silu(x):
    return jax.nn.silu(x)

def _sigmoid(x):
    return jax.nn.sigmoid(x)

def _layernorm(x, axis=-1, eps=1e-05):
    m = jnp.mean(x, axis=axis, keepdims=True)
    v = jnp.var(x, axis=axis, keepdims=True)
    return (x - m) / jnp.sqrt(v + eps)

def _scatter_add(tgt, idx, src, axis=0):
    return tgt.at[idx].add(src)

def _segment_sum(src, seg, n):
    return jax.ops.segment_sum(src, seg, n)
kernel_name = 'mk_flamingo_gated_d1_seqx_r8_5c7a4e'

def setup_inputs(seed: int=0):
    np.random.seed(seed)
    _w = jnp.asarray

    def _rec_inputs():
        import jax
        import jax.numpy as jnp
        _rk = jax.random.key(seed)
        x = 0.5 + 0.2887 * jax.random.normal(jax.random.fold_in(_rk, 1), (4, 256, 256), jnp.float32)
        _lenS = 256 - jax.random.randint(jax.random.fold_in(_rk, 7), (4,), 0, max(1, 256 // 4) + 1, jnp.int32)
        _lenS2 = 256 - jax.random.randint(jax.random.fold_in(_rk, 8), (4,), 0, max(1, 256 // 4) + 1, jnp.int32)
        _ctx_512P = jax.random.normal(jax.random.fold_in(_rk, 11), (4, 16, 64), jnp.float32)
        _ctx_512c = jax.random.dirichlet(jax.random.fold_in(_rk, 511), 0.3 * jnp.ones((16,), jnp.float32), (4, 256))
        _ctx_512t = jnp.einsum('bsk,bkd->bsd', _ctx_512c, _ctx_512P)
        _ctx_512t = _ctx_512t * jax.lax.rsqrt(jnp.mean(jnp.square(_ctx_512t)) + 1e-12) * 0.953939
        ctx_512 = -0.000392918 + 0.999932 * (_ctx_512t + 0.3 * jax.random.normal(jax.random.fold_in(_rk, 611), (4, 256, 64), jnp.float32))
        _g = jax.random.normal(jax.random.fold_in(_rk, 9001), (2, 1), jnp.float32)
        _g = jnp.sign(_g) * jnp.maximum(jnp.abs(_g), 1.0) + (_g == 0) * 1.0
        g_xattn = _g[0]
        g_ffn = _g[1]
        return (x, ctx_512, g_xattn, g_ffn)
    x, ctx_512, g_xattn, g_ffn = _rec_inputs()

    def _L0_xattn_setup():
        import jax, jax.numpy as jnp
        import numpy as np
        B, N, D = (16, 256, 64)
        H = 4
        TOP_K_RATIO = 0.3
        key = jax.random.key(seed)
        k1, k2, k3, k4 = jax.random.split(key, 4)
        h = jax.random.normal(k1, (B, N, D), dtype=jnp.float32)
        adj_raw = jax.random.uniform(k2, (B, N, N), dtype=jnp.float32)
        lim = 1.0 / np.sqrt(D)
        Wq = jax.random.uniform(k3, (D, D), minval=-lim, maxval=lim, dtype=jnp.float32)
        Wk = jax.random.uniform(k4, (D, D), minval=-lim, maxval=lim, dtype=jnp.float32)
        gamma_raw = jnp.float32(-0.85)
        return {'h': h, 'adj_raw': adj_raw, 'Wq': Wq, 'Wk': Wk, 'gamma_raw': gamma_raw}
    _L0_xattn_all = _L0_xattn_setup()
    _L0_xattn_in = {k: v for k, v in _L0_xattn_all.items() if k in ('Wq', 'Wk', 'gamma_raw')}
    del _L0_xattn_all

    def _L0_ffn_setup():
        import jax, jax.numpy as jnp
        import numpy as np
        B, S, H = (2, 128, 256)
        E, K = (8, 2)
        I = 176
        IS = 704
        WSCALE = 0.02
        key = jax.random.key(seed)
        ks = jax.random.split(key, 9)
        f32 = jnp.float32
        return {'hidden_states': jax.random.normal(ks[0], (B, S, H), dtype=f32), 'gate_w': jax.random.normal(ks[1], (E, H), dtype=f32) * WSCALE, 'w_gate': jax.random.normal(ks[2], (E, H, I), dtype=f32) * WSCALE, 'w_up': jax.random.normal(ks[3], (E, H, I), dtype=f32) * WSCALE, 'w_down': jax.random.normal(ks[4], (E, I, H), dtype=f32) * WSCALE, 'sw_gate': jax.random.normal(ks[5], (H, IS), dtype=f32) * WSCALE, 'sw_up': jax.random.normal(ks[6], (H, IS), dtype=f32) * WSCALE, 'sw_down': jax.random.normal(ks[7], (IS, H), dtype=f32) * WSCALE, 'shared_gate_w': jax.random.normal(ks[8], (H, 1), dtype=f32) * WSCALE}
    _L0_ffn_all = _L0_ffn_setup()
    _L0_ffn_in = {k: v for k, v in _L0_ffn_all.items() if k in ('gate_w', 'w_gate', 'w_up', 'w_down', 'sw_gate', 'sw_up', 'sw_down', 'shared_gate_w')}
    del _L0_ffn_all
    return {'x': x, 'ctx_512': ctx_512, 'g_xattn': g_xattn, 'g_ffn': g_ffn, 'L0_xattn_Wq': _L0_xattn_in['Wq'], 'L0_xattn_Wk': _L0_xattn_in['Wk'], 'L0_xattn_gamma_raw': _L0_xattn_in['gamma_raw'], 'L0_ffn_gate_w': _L0_ffn_in['gate_w'], 'L0_ffn_w_gate': _L0_ffn_in['w_gate'], 'L0_ffn_w_up': _L0_ffn_in['w_up'], 'L0_ffn_w_down': _L0_ffn_in['w_down'], 'L0_ffn_sw_gate': _L0_ffn_in['sw_gate'], 'L0_ffn_sw_up': _L0_ffn_in['sw_up'], 'L0_ffn_sw_down': _L0_ffn_in['sw_down'], 'L0_ffn_shared_gate_w': _L0_ffn_in['shared_gate_w']}

def reference(x, ctx_512, g_xattn, g_ffn, L0_xattn_Wq, L0_xattn_Wk, L0_xattn_gamma_raw, L0_ffn_gate_w, L0_ffn_w_gate, L0_ffn_w_up, L0_ffn_w_down, L0_ffn_sw_gate, L0_ffn_sw_up, L0_ffn_sw_down, L0_ffn_shared_gate_w):
    import jax
    import jax.numpy as jnp

    def _L0_xattn_ref(h, adj_raw, Wq, Wk, gamma_raw):
        import jax, jax.numpy as jnp
        import numpy as np
        B, N, D = (16, 256, 64)
        H = 4
        TOP_K_RATIO = 0.3
        b, n, dm = h.shape
        d = dm // H
        Q = (h @ Wq.T).reshape(b, n, H, d).transpose(0, 2, 1, 3)
        K = (h @ Wk.T).reshape(b, n, H, d).transpose(0, 2, 1, 3)
        sim = jnp.einsum('bhnd,bhmd->bnm', Q, K) / (jnp.sqrt(jnp.float32(d)) * H)
        k = max(1, int(n * TOP_K_RATIO))
        topk_vals = jax.lax.top_k(sim, k)[0]
        threshold = topk_vals[:, :, -1:]
        sparse_mask = (sim >= threshold).astype(sim.dtype)
        A_learned = jax.nn.sigmoid(sim) * sparse_mask
        A_learned = (A_learned + jnp.swapaxes(A_learned, -1, -2)) * 0.5
        gamma = jax.nn.sigmoid(gamma_raw)
        return (1.0 - gamma) * adj_raw + gamma * A_learned

    def _L0_ffn_ref(hidden_states, gate_w, w_gate, w_up, w_down, sw_gate, sw_up, sw_down, shared_gate_w):
        import jax, jax.numpy as jnp
        import numpy as np
        B, S, H = (2, 128, 256)
        E, K = (8, 2)
        I = 176
        IS = 704
        WSCALE = 0.02
        x = hidden_states
        logits = jnp.einsum('bsh,eh->bse', x, gate_w)
        probs = jax.nn.softmax(logits, axis=-1)
        top_w, top_i = jax.lax.top_k(probs, K)
        top_w = top_w / jnp.sum(top_w, axis=-1, keepdims=True)
        onehot = jax.nn.one_hot(top_i, E, dtype=x.dtype)
        combine = jnp.einsum('bsk,bske->bse', top_w, onehot)
        g = jnp.einsum('bsh,ehi->besi', x, w_gate)
        u = jnp.einsum('bsh,ehi->besi', x, w_up)
        h = jax.nn.silu(g) * u
        expert_out = jnp.einsum('besi,eih->besh', h, w_down)
        moe_out = jnp.einsum('besh,bse->bsh', expert_out, combine)
        sh = jax.nn.silu(x @ sw_gate) * (x @ sw_up)
        shared_out = sh @ sw_down
        shared_gate = jax.nn.sigmoid(x @ shared_gate_w)
        return moe_out + shared_out * shared_gate
    x = x + jnp.tanh(g_xattn[0]) * _L0_xattn_ref(ctx_512, _layernorm(x, axis=-1), L0_xattn_Wq, L0_xattn_Wk, L0_xattn_gamma_raw)
    x = x + jnp.tanh(g_ffn[0]) * _L0_ffn_ref(_layernorm(x, axis=-1), L0_ffn_gate_w, L0_ffn_w_gate, L0_ffn_w_up, L0_ffn_w_down, L0_ffn_sw_gate, L0_ffn_sw_up, L0_ffn_sw_down, L0_ffn_shared_gate_w)
    return x

_drawn_inputs = setup_inputs


def setup_inputs(seed=0):
    import zlib

    import numpy as np

    out = dict(_drawn_inputs(seed))
    spreads = {}
    factors = {'L0_ffn_gate_w': 6.78,
     'L0_ffn_w_gate': 5.976,
     'L0_ffn_w_up': 5.918,
     'L0_ffn_w_down': 5.914,
     'L0_ffn_sw_gate': 4.158,
     'L0_ffn_sw_up': 4.136,
     'L0_ffn_sw_down': 4.135,
     'L0_ffn_shared_gate_w': 8.0}
    for name, (base, spread) in spreads.items():
        noise = np.random.default_rng([zlib.crc32(name.encode()), seed]).standard_normal(out[name].shape)
        drawn = base * np.exp(spread * noise) if base else spread * noise
        out[name] = jnp.asarray(drawn.astype(out[name].dtype))
    for name, factor in factors.items():
        out[name] = (out[name] * factor).astype(out[name].dtype)
    return out
```

```python
from contextlib import ExitStack

import concourse.bass as bass
from concourse import mybir

ALU = mybir.AluOpType
ACT = mybir.ActivationFunctionType
F32 = mybir.dt.float32
F32R = mybir.dt.float32r
U32 = mybir.dt.uint32

P = 128
NB, NTOK, D, DC = 4, 256, 256, 64
KD = D // P
E, EI, SI = 8, 176, 704
MOE_CH = E * EI // P
CHUNKS = (E * EI + SI) // P
TAIL = E * EI + SI - CHUNKS * P
PAIRS = CHUNKS // 2
SLOTS = PAIRS + 1
TOPK = int(NTOK * 0.3)
ROUNDS = (TOPK + 7) // 8
EPS = 1e-5
NSEL = MOE_CH + 1
CW = 10
CB_WRITES = (MOE_CH + 1) // 2 + 1
BIG = 3.0e38
assert 2 * PAIRS == CHUNKS and TAIL == 64 and NTOK == 2 * P

PIECE = 1024
PIECES = []
for _q in range(CHUNKS // 4):
    PIECES += [("gu", 4 * _q), ("gu", 4 * _q + 2), ("wd", 4 * _q)]
PIECES += [("tail", CHUNKS)]
WCOLS = PIECE * (len(PIECES) - 1) + 512
RING = 5
EARLY = 7


def gu_at(chunk):
    n = PIECES.index(("tail", CHUNKS) if chunk == CHUNKS else ("gu", chunk - chunk % 2))
    return n, n * PIECE + (0 if chunk == CHUNKS else 512 * (chunk % 2))


def wd_at(chunk):
    n = PIECES.index(("tail", CHUNKS) if chunk == CHUNKS else ("wd", chunk - chunk % 4))
    return n, n * PIECE + (256 if chunk == CHUNKS else 256 * (chunk % 4))


def build(nc, x, ctx_t, wqk, scal, gw, sel, const, wpack, out):
    x_v = x.rearrange("b (r p) d -> p (b r) d", p=P)
    out_v = out.rearrange("b (r p) d -> p (b r) d", p=P)
    NSLOT = NB * SLOTS

    with ExitStack() as ctx:
        def sb(name, shape, dt=F32):
            return ctx.enter_context(nc.sbuf_tensor(name, shape, dt))

        def sem(name):
            return ctx.enter_context(nc.semaphore(name))

        def bank(name):
            return ctx.enter_context(nc.psum_tensor(name, [P, 512], F32))

        gate_ps = [bank("gate0"), bank("gate1")]
        up_ps = [bank("up0"), bank("up1")]
        cb_ps = bank("cb")
        down_ps = [bank("down0"), bank("down1")]
        misc_ps = bank("misc")

        xs = sb("xs", [P, 2 * NB, D])
        ctxT = sb("ctxT", [DC, NB * NTOK])
        wqk_sb = sb("wqk_sb", [DC, 2 * DC])
        m_sb = sb("m_sb", [DC, DC])
        hmT = sb("hmT", [DC, NB * NTOK])
        const_sb = sb("const_sb", [P, P + 9])
        ident = const_sb[:, 0:P]
        iota8 = const_sb[:, P:P + 8]
        minus_half = const_sb[:, P + 8:P + 9]
        scal_sb = sb("scal_sb", [P, 3])
        tscal = sb("tscal", [P, 3])
        coef = sb("coef", [P, 4])
        c_res, c_adj, c_ffn = coef[:, 1:2], coef[:, 2:3], tscal[:, 1:2]
        gw_raw = sb("gw_raw", [P, KD * CW])
        gw_hi = sb("gw_hi", [P, KD * CW], F32R)
        gw_lo = sb("gw_lo", [P, KD * CW], F32R)
        sel_raw = sb("sel_raw", [2 * CW, NSEL * P])
        sel_r = sb("sel_r", [2 * CW, NSEL * P], F32R)
        raw = sb("raw", [P, RING, PIECE])
        w_hi = sb("w_hi", [P, WCOLS], F32R)
        w_lo = sb("w_lo", [P, WCOLS], F32R)
        sim = sb("sim", [P, 2, NTOK])
        work = sb("work", [P, 2, NTOK])
        top8 = sb("top8", [P, 2, 8])
        th1 = sb("th1", [P, 2, NTOK])
        adj = sb("adj", [P, 2, NTOK])
        st1 = sb("st1", [P, 2, 6])
        mv1 = sb("mv1", [P, NB, 2, 2])
        ln1 = sb("ln1", [P, NB, 4, 2])
        st2 = sb("st2", [P, 2, 6])
        mv2 = sb("mv2", [P, 2, 2])
        rs2 = sb("rs2", [P, 2, 2])
        y = sb("y", [P, 2, D])
        yT_hi = sb("yT_hi", [P, NB, 2 * NTOK], F32R)
        yT_lo = sb("yT_lo", [P, NB, 2 * NTOK], F32R)
        lg = sb("lg", [P, 2, CW])
        lmax = sb("lmax", [P, 2, 8])
        lidx = sb("lidx", [P, 2, 8], U32)
        lidf = sb("lidf", [P, 2, 8])
        dz = sb("dz", [P, 2, 2])
        tdz = sb("tdz", [P, 2, 2])
        wts = sb("wts", [P, 2, 3])
        pick = sb("pick", [P, 2, 8])
        comb = sb("comb", [P, 2, CW])
        comb_split = sb("comb_split", [P, 2, 2 * CW])
        cT = sb("cT", [2 * CW, NB * NTOK], F32R)
        act_in = sb("act_in", [P, 1])
        act_out = sb("act_out", [P, 1])
        silu_sb = sb("silu_sb", [P, 2, 512])
        h32 = sb("h32", [P, 2, 512])
        h_hi = sb("h_hi", [P, 3, 512], F32R)
        h_lo = sb("h_lo", [P, 3, 512], F32R)
        comb_hi = sb("comb_hi", [P, 2, CW], F32R)

        ctx_in, wqk_in, scal_in, gw_in, sel_in, const_in = (sem(n) for n in (
            "ctx_in", "wqk_in", "scal_in", "gw_in", "sel_in", "const_in"))
        x_in = [sem(f"x_in{b}") for b in range(NB)]
        raw_in = [sem(f"raw_in{s}") for s in range(RING)]
        out_sent = sem("out_sent")
        m_ready, hm_ready, sim_ready, adjT_ready, yT_ready, logit_ready, cT_ready = (sem(n) for n in (
            "m_ready", "hm_ready", "sim_ready", "adjT_ready", "yT_ready", "logit_ready", "cT_ready"))
        gu_ready, cb_ready, down_done = sem("gu_ready"), sem("cb_ready"), sem("down_done")
        tscal_done, m_copied, hm_copied, sim_copied, tanh_done, base_done = (sem(n) for n in (
            "tscal_done", "m_copied", "hm_copied", "sim_copied", "tanh_done", "base_done"))
        yhi_done, tdz_done, cT_copied, silu_done, hhi_done, whi_done = (sem(n) for n in (
            "yhi_done", "tdz_done", "cT_copied", "silu_done", "hhi_done", "whi_done"))
        zeroed, xstat_step, mv1_done, topk_step, adj_done, x2a_done, x2_done = (sem(n) for n in (
            "zeroed", "xstat_step", "mv1_done", "topk_step", "adj_done", "x2a_done", "x2_done"))
        stat2_step, mv2_done, y_done, ylo_done, route_step, dz_done, comb_done = (sem(n) for n in (
            "stat2_step", "mv2_done", "y_done", "ylo_done", "route_step", "dz_done", "comb_done"))
        t2_done, t3_done, out_done = sem("t2_done"), sem("t3_done"), sem("out_done")
        consts_split, gwhi_done, coef_step, ln1_step, ln1_done, th1_done = (sem(n) for n in (
            "consts_split", "gwhi_done", "coef_step", "ln1_step", "ln1_done", "th1_done"))
        rs2_step, rs2_done, wlo_done, hlo_done = (sem(n) for n in (
            "rs2_step", "rs2_done", "wlo_done", "hlo_done"))

        block = ctx.enter_context(nc.Block())

        @block.sync
        def _(sp):
            sp.dma_start(wqk_sb[:, :], wqk).then_inc(wqk_in, 16)
            sp.dma_start(xs[:, 0:2, :], x_v[:, 0:2, :]).then_inc(x_in[0], 16)
            sp.dma_start(raw[:, 0, :], wpack[:, 0:PIECE]).then_inc(raw_in[0], 16)
            sp.dma_start(xs[:, 2:4, :], x_v[:, 2:4, :]).then_inc(x_in[1], 16)
            for n in range(1, len(PIECES)):
                if n >= RING:
                    sp.wait_ge(wlo_done, n - RING + 1)
                w = min(PIECE, WCOLS - n * PIECE)
                sp.dma_start(raw[:, n % RING, 0:w], wpack[:, n * PIECE:n * PIECE + w]).then_inc(raw_in[n % RING], 16)
                if n in (3, 4):
                    b = n - 1
                    sp.dma_start(xs[:, 2 * b:2 * b + 2, :], x_v[:, 2 * b:2 * b + 2, :]).then_inc(x_in[b], 16)
            for b in range(NB):
                sp.wait_ge(out_done, b + 1)
                sp.dma_start(out_v[:, 2 * b:2 * b + 2, :], xs[:, 2 * b:2 * b + 2, :]).then_inc(out_sent, 16)
            sp.wait_ge(out_sent, 16 * NB)

        @block.tensor
        def _(pe):
            def similarity(b):
                pe.wait_ge(hm_copied, b + 1)
                for r in range(2):
                    i = 2 * b + r
                    last = pe.matmul(misc_ps[:, r * NTOK:(r + 1) * NTOK], hmT[:, i * P:(i + 1) * P],
                                     ctxT[:, b * NTOK:(b + 1) * NTOK], start=True, stop=True)
                last.then_inc(sim_ready, 1)

            def transpose_adj(b):
                pe.wait_ge(adj_done, 2 * (b + 1))
                for r in range(2):
                    for c in range(2):
                        last = pe.transpose(misc_ps[:, r * NTOK + c * P:r * NTOK + (c + 1) * P],
                                            adj[:, c, r * P:(r + 1) * P], ident)
                last.then_inc(adjT_ready, 1)

            def transpose_y(b):
                pe.wait_ge(y_done, 2 * (b + 1))
                for k in range(KD):
                    for r in range(2):
                        last = pe.transpose(misc_ps[:, k * NTOK + r * P:k * NTOK + (r + 1) * P],
                                            y[:, r, k * P:(k + 1) * P], ident)
                last.then_inc(yT_ready, 1)

            def logits(b):
                pe.wait_ge(yhi_done, b + 1)
                pe.wait_ge(ylo_done, b + 1)
                pe.wait_ge(consts_split, 3)
                for r in range(2):
                    for k in range(KD):
                        at = slice(k * NTOK + r * P, k * NTOK + (r + 1) * P)
                        gk = slice(k * CW, (k + 1) * CW)
                        for n, (a, w) in enumerate(((yT_hi, gw_hi), (yT_hi, gw_lo), (yT_lo, gw_hi))):
                            last = pe.matmul(misc_ps[:, r * CW:(r + 1) * CW], a[:, b, at], w[:, gk],
                                             start=(k == 0 and n == 0), stop=(k == KD - 1 and n == 2))
                last.then_inc(logit_ready, 1)

            def transpose_comb(b):
                pe.wait_ge(comb_done, b + 1)
                for r in range(2):
                    last = pe.transpose(misc_ps[0:2 * CW, r * P:(r + 1) * P], comb_split[:, r, :], ident)
                last.then_inc(cT_ready, 1)

            def gate_up(s):
                g, m = s // SLOTS, s % SLOTS
                if m == 0:
                    pe.wait_ge(yhi_done, g + 1)
                    pe.wait_ge(ylo_done, g + 1)
                if s >= 2:
                    pe.wait_ge(silu_done, s - 1)
                    pe.wait_ge(t2_done, s - 1)
                chunks = (2 * m, 2 * m + 1) if m < PAIRS else (CHUNKS,)
                for q, c in enumerate(chunks):
                    n, col = gu_at(c)
                    if g == 0:
                        pe.wait_ge(whi_done, n + 1)
                        pe.wait_ge(wlo_done, n + 1)
                    for half, dst in enumerate((gate_ps, up_ps) if m < PAIRS else (gate_ps,)):
                        for k in range(KD):
                            wk = slice(col + (half * KD + k) * P, col + (half * KD + k + 1) * P)
                            yk = slice(k * NTOK, (k + 1) * NTOK)
                            for t, (w, a) in enumerate(((w_hi, yT_hi), (w_hi, yT_lo), (w_lo, yT_hi))):
                                last = pe.matmul(dst[s % 2][:, q * NTOK:(q + 1) * NTOK], w[:, wk], a[:, g, yk],
                                                 start=(k == 0 and t == 0), stop=(k == KD - 1 and t == 2))
                last.then_inc(gu_ready, 1)

            def spread_c(s):
                g, m = s // SLOTS, s % SLOTS
                if m >= CB_WRITES:
                    return
                if m == 0:
                    pe.wait_ge(cT_copied, g + 1)
                    pe.wait_ge(consts_split, 1)
                if s >= 1:
                    pe.wait_ge(t3_done, s)
                for q in range(2):
                    j = min(2 * m + q, MOE_CH)
                    last = pe.matmul(cb_ps[:, q * NTOK:(q + 1) * NTOK], sel_r[:, j * P:(j + 1) * P],
                                     cT[:, g * NTOK:(g + 1) * NTOK], start=True, stop=True)
                last.then_inc(cb_ready, 1)

            def down(s):
                g, m = s // SLOTS, s % SLOTS
                pe.wait_ge(hhi_done, s + 1)
                pe.wait_ge(hlo_done, s + 1)
                if m == 0 and g >= 2:
                    pe.wait_ge(out_done, g - 1)
                chunks = (2 * m, 2 * m + 1) if m < PAIRS else (CHUNKS,)
                for q, c in enumerate(chunks):
                    n, col = wd_at(c)
                    if g == 0:
                        pe.wait_ge(whi_done, n + 1)
                        pe.wait_ge(wlo_done, n + 1)
                    rows = slice(0, P) if c < CHUNKS else slice(P - TAIL, P)
                    wc = slice(col, col + D)
                    for r in range(2):
                        at = slice(q * NTOK + r * P, q * NTOK + (r + 1) * P)
                        for t, (h, w) in enumerate(((h_hi, w_hi), (h_hi, w_lo), (h_lo, w_hi))):
                            last = pe.matmul(down_ps[g % 2][:, r * D:(r + 1) * D], h[rows, s % 3, at], w[rows, wc],
                                             start=(c == 0 and r == 0 and t == 0), stop=(c == CHUNKS and t == 2),
                                             skip_group_check=True)
                last.then_inc(down_done, 1)

            pe.wait_ge(wqk_in, 16)
            pe.matmul(up_ps[0][0:DC, 0:DC], wqk_sb[:, 0:DC], wqk_sb[:, DC:2 * DC],
                      start=True, stop=True).then_inc(m_ready, 1)
            pe.wait_ge(m_copied, 1)
            pe.wait_ge(ctx_in, 16)
            for b, hm_ps in enumerate((up_ps[1], gate_ps[0], gate_ps[1], up_ps[0])):
                pe.matmul(hm_ps[0:DC, 0:NTOK], m_sb[:, :], ctxT[:, b * NTOK:(b + 1) * NTOK],
                          start=True, stop=True).then_inc(hm_ready, 1)
                if b == 0:
                    similarity(0)
            pe.wait_ge(const_in, 16)
            transpose_adj(0)
            pe.wait_ge(x2_done, 1)
            similarity(1)
            pe.wait_ge(sim_copied, 2)
            transpose_y(0)
            logits(0)
            pe.wait_ge(hm_copied, NB)
            for s in range(NSLOT):
                g, m = s // SLOTS, s % SLOTS
                gate_up(s)
                if m == 0:
                    transpose_comb(g)
                if m == 5 and g + 1 < NB:
                    pe.wait_ge(cT_copied, g + 1)
                    transpose_adj(g + 1)
                if m == 6 and g + 2 < NB:
                    pe.wait_ge(x2_done, g + 2)
                    similarity(g + 2)
                if m == 7 and g + 1 < NB:
                    if g + 2 < NB:
                        pe.wait_ge(sim_copied, g + 3)
                    transpose_y(g + 1)
                if m == 8 and g + 1 < NB:
                    logits(g + 1)
                if s >= 2:
                    down(s - 2)
                spread_c(s)
            down(NSLOT - 2)
            down(NSLOT - 1)

        @block.scalar
        def _(act):
            def weights_hi(n):
                w = min(PIECE, WCOLS - n * PIECE)
                act.wait_ge(raw_in[n % RING], 16 * (n // RING + 1))
                act.activation(w_hi[:, n * PIECE:n * PIECE + w], raw[:, n % RING, 0:w], ACT.Copy).then_inc(whi_done, 1)

            def copy_sim(b):
                act.wait_ge(sim_ready, b + 1)
                if b >= 1:
                    act.wait_ge(adj_done, 2 * b)
                act.activation(sim[:, :, :].rearrange("p r n -> p (r n)"), misc_ps[:, :], ACT.Copy).then_inc(sim_copied, 1)
                act.wait_ge(sim_copied, b + 1)
                act.activation(th1[:, :, :], sim[:, :, :], ACT.Tanh, scale=1.0 / 32).then_inc(tanh_done, 1)

            def residual_base(b):
                act.wait_ge(ln1_done, b + 1)
                for r in range(2):
                    act.activation(xs[:, 2 * b + r, :], xs[:, 2 * b + r, :], ACT.Identity,
                                   bias=ln1[:, b, 3, r:r + 1], scale=ln1[:, b, 2, r:r + 1]).then_inc(base_done, 1)

            def split_y(b):
                act.wait_ge(yT_ready, b + 1)
                act.activation(yT_hi[:, b, :], misc_ps[:, :], ACT.Copy).then_inc(yhi_done, 1)

            def silu(s):
                act.wait_ge(gu_ready, s + 1)
                if s >= 2:
                    act.wait_ge(t2_done, s - 1)
                if s % SLOTS < PAIRS:
                    act.activation(silu_sb[:, s % 2, :], gate_ps[s % 2][:, :], ACT.Silu).then_inc(silu_done, 1)
                else:
                    act.activation(silu_sb[P - TAIL:P, s % 2, 0:NTOK], gate_ps[s % 2][0:TAIL, 0:NTOK],
                                   ACT.Silu).then_inc(silu_done, 1)

            def hidden_hi(s):
                act.wait_ge(t3_done, s + 1)
                if s >= 3:
                    act.wait_ge(down_done, s - 2)
                rows, cols = (slice(0, P), 512) if s % SLOTS < PAIRS else (slice(P - TAIL, P), NTOK)
                act.activation(h_hi[rows, s % 3, 0:cols], h32[rows, s % 2, 0:cols], ACT.Copy).then_inc(hhi_done, 1)

            act.dma_start(ctxT[:, :], ctx_t).then_inc(ctx_in, 16)
            act.dma_start(scal_sb[:, :], scal).then_inc(scal_in, 16)
            act.dma_start(const_sb[:, :], const).then_inc(const_in, 16)
            act.dma_start(gw_raw[:, :], gw).then_inc(gw_in, 16)
            act.dma_start(sel_raw[:, :], sel).then_inc(sel_in, 16)
            act.wait_ge(zeroed, 1)
            act.activation(act_out[:, :], act_in[:, :], ACT.Silu)
            act.wait_ge(m_ready, 1)
            act.activation(m_sb[:, :], up_ps[0][0:DC, 0:DC], ACT.Copy).then_inc(m_copied, 1)
            hm_banks = (up_ps[1], gate_ps[0], gate_ps[1], up_ps[0])
            for b in range(NB):
                act.wait_ge(hm_ready, b + 1)
                act.activation(hmT[:, b * NTOK:(b + 1) * NTOK], hm_banks[b][0:DC, 0:NTOK], ACT.Copy).then_inc(hm_copied, 1)
                if b == 0:
                    copy_sim(0)
            act.wait_ge(scal_in, 16)
            act.activation(tscal[:, 0:2], scal_sb[:, 0:2], ACT.Tanh).then_inc(tscal_done, 1)
            act.activation(tscal[:, 2:3], scal_sb[:, 2:3], ACT.Tanh, scale=0.5).then_inc(tscal_done, 1)
            weights_hi(0)
            residual_base(0)
            for n in range(1, EARLY):
                weights_hi(n)
            residual_base(1)
            copy_sim(1)
            split_y(0)
            for s in range(NSLOT):
                g, m = s // SLOTS, s % SLOTS
                if m == 0:
                    act.wait_ge(dz_done, g + 1)
                    act.activation(tdz[:, :, :], dz[:, :, :], ACT.Tanh, scale=0.5).then_inc(tdz_done, 1)
                silu(s)
                if m == 0:
                    act.wait_ge(cT_ready, g + 1)
                    act.activation(cT[:, g * NTOK:(g + 1) * NTOK], misc_ps[0:2 * CW, 0:NTOK], ACT.Copy).then_inc(cT_copied, 1)
                if g == 0 and EARLY + m < len(PIECES):
                    weights_hi(EARLY + m)
                if m == 3 and g >= 1 and g + 1 < NB:
                    residual_base(g + 1)
                if m == 6 and g + 2 < NB:
                    copy_sim(g + 2)
                if m == 7 and g + 1 < NB:
                    split_y(g + 1)
                hidden_hi(s)

        @block.vector
        def _(dve):
            def stats(tile, st, mv, step, done, count):
                for r in range(2):
                    dve.bn_stats(st[:, r, :], tile[:, r, :]).then_inc(step, 1)
                for r in range(2):
                    dve.wait_ge(step, 2 * count + r + 1)
                    dve.bn_aggr(mv[:, r, :], st[:, r, :]).then_inc(done, 1)

            def x_stats(b):
                dve.wait_ge(x_in[b], 16)
                if b >= 1:
                    dve.wait_ge(mv1_done, 2 * b)
                stats(xs[:, 2 * b:2 * b + 2, :], st1, mv1[:, b, :, :], xstat_step, mv1_done, b)

            def topk_rounds(b, first, end):
                def follow(n):
                    if n >= 2:
                        dve.wait_ge(topk_step, n - 1)

                for k in range(first, end):
                    if k == 0:
                        dve.wait_ge(sim_copied, b + 1)
                    n = b * (4 * ROUNDS - 2) + 4 * k
                    for r in range(2):
                        follow(n + r)
                        dve.max(top8[:, r, :], (sim if k == 0 else work)[:, r, :]).then_inc(topk_step, 1)
                    if k < ROUNDS - 1:
                        for r in range(2):
                            follow(n + 2 + r)
                            dve.match_replace(work[:, r, :], top8[:, r, :], (sim if k == 0 else work)[:, r, :],
                                              -BIG).then_inc(topk_step, 1)

            def adjacency(b):
                kth = TOPK - 8 * (ROUNDS - 1) - 1
                dve.wait_ge(th1_done, b + 1)
                if b >= 1:
                    dve.wait_ge(adjT_ready, b)
                for r in range(2):
                    dve.wait_ge(topk_step, (b + 1) * (4 * ROUNDS - 2) - 1 + r)
                    dve.scalar_tensor_tensor(adj[:, r, :], sim[:, r, :], top8[:, r, kth:kth + 1], th1[:, r, :],
                                             ALU.is_ge, ALU.mult).then_inc(adj_done, 1)
                dve.wait_ge(adj_done, 2 * (b + 1))
                dve.wait_ge(base_done, 2 * (b + 1))
                xb = xs[:, 2 * b:2 * b + 2, :]
                dve.scalar_tensor_tensor(xb, adj[:, :, :], c_adj, xb, ALU.mult, ALU.add).then_inc(x2a_done, 1)

            def finish_x2(b):
                xb = xs[:, 2 * b:2 * b + 2, :]
                dve.wait_ge(x2a_done, b + 1)
                dve.wait_ge(adjT_ready, b + 1)
                dve.scalar_tensor_tensor(xb, misc_ps[:, :].rearrange("p (r n) -> p r n", r=2), c_adj, xb,
                                         ALU.mult, ALU.add).then_inc(x2_done, 1)
                dve.wait_ge(x2_done, b + 1)
                stats(xb, st2, mv2, stat2_step, mv2_done, b)

            def normalise(b):
                dve.wait_ge(rs2_done, b + 1)
                if b >= 1:
                    dve.wait_ge(yT_ready, b)
                for r in range(2):
                    dve.tensor_scalar(y[:, r, :], xs[:, 2 * b + r, :], mv2[:, r, 0:1], rs2[:, 1, r:r + 1],
                                      ALU.subtract, ALU.mult).then_inc(y_done, 1)

            def y_lo(b):
                dve.wait_ge(yhi_done, b + 1)
                dve.tensor_tensor(yT_lo[:, b, :], misc_ps[:, :], yT_hi[:, b, :].bitcast(F32),
                                  ALU.subtract).then_inc(ylo_done, 1)

            ROUTE = 16

            def route_first(b):
                n = b * ROUTE
                dve.wait_ge(logit_ready, b + 1)
                dve.tensor_copy(lg[:, :, :], misc_ps[:, 0:2 * CW].rearrange("p (r e) -> p r e", r=2)).then_inc(route_step, 1)
                dve.wait_ge(route_step, n + 1)
                for r in range(2):
                    dve.max(lmax[:, r, :], lg[:, r, 0:E]).then_inc(route_step, 1)
                dve.wait_ge(route_step, n + 3)
                dve.tensor_tensor(dz[:, :, 0:1], lmax[:, :, 0:1], lmax[:, :, 1:2], ALU.subtract).then_inc(route_step, 1)
                dve.wait_ge(route_step, n + 4)
                dve.tensor_copy(dz[:, :, 1:2], lg[:, :, E:E + 1]).then_inc(dz_done, 1)
                for r in range(2):
                    dve.max_index(lidx[:, r, :], lmax[:, r, :], lg[:, r, 0:E]).then_inc(route_step, 1)
                dve.wait_ge(route_step, n + 6)
                dve.tensor_copy(lidf[:, :, :], lidx[:, :, :]).then_inc(route_step, 1)

            def route_second(b):
                n = b * ROUTE + 7
                dve.wait_ge(tdz_done, b + 1)
                dve.tensor_scalar(wts[:, :, 0:2], tdz[:, :, :], 0.5, 0.5, ALU.mult, ALU.add).then_inc(route_step, 1)
                dve.tensor_scalar(wts[:, :, 2:3], tdz[:, :, 0:1], -0.5, 0.5, ALU.mult, ALU.add).then_inc(route_step, 1)
                dve.wait_ge(route_step, n + 2)
                for r in range(2):
                    dve.tensor_scalar(pick[:, r, :], iota8, lidf[:, r, 0:1], wts[:, r, 0:1],
                                      ALU.is_equal, ALU.mult).then_inc(route_step, 1)
                    dve.tensor_scalar(comb[:, r, 0:E], iota8, lidf[:, r, 1:2], wts[:, r, 2:3],
                                      ALU.is_equal, ALU.mult).then_inc(route_step, 1)
                dve.tensor_copy(comb[:, :, E:E + 1], wts[:, :, 1:2]).then_inc(route_step, 1)
                dve.wait_ge(route_step, n + 7)
                dve.tensor_tensor(comb[:, :, 0:E], comb[:, :, 0:E], pick[:, :, :], ALU.add).then_inc(route_step, 1)
                dve.wait_ge(route_step, n + 8)
                dve.tensor_copy(comb_hi[:, :, :], comb[:, :, :]).then_inc(route_step, 1)
                dve.wait_ge(route_step, n + 9)
                if b >= 1:
                    dve.wait_ge(cT_ready, b)
                dve.tensor_copy(comb_split[:, :, 0:CW], comb_hi[:, :, :].bitcast(F32))
                dve.tensor_tensor(comb_split[:, :, CW:2 * CW], comb[:, :, :], comb_hi[:, :, :].bitcast(F32),
                                  ALU.subtract).then_inc(comb_done, 1)

            def hidden(s):
                g, m = s // SLOTS, s % SLOTS
                rows, cols, up = (slice(0, P), 512, up_ps) if m < PAIRS else (slice(P - TAIL, P), NTOK, gate_ps)
                dve.wait_ge(silu_done, s + 1)
                if s >= 2:
                    dve.wait_ge(hlo_done, s - 1)
                h = h32[rows, s % 2, 0:cols]
                dve.tensor_tensor(h, silu_sb[rows, s % 2, 0:cols], up[s % 2][rows, 0:cols], ALU.mult).then_inc(t2_done, 1)
                dve.wait_ge(t2_done, s + 1)
                dve.wait_ge(cb_ready, g * CB_WRITES + min(m + 1, CB_WRITES))
                dve.tensor_tensor(h, h, cb_ps[rows, 0:cols], ALU.mult).then_inc(t3_done, 1)

            def result(b):
                xb = xs[:, 2 * b:2 * b + 2, :]
                dve.wait_ge(down_done, SLOTS * (b + 1))
                dve.scalar_tensor_tensor(xb, down_ps[b % 2][:, :].rearrange("p (r n) -> p r n", r=2), c_ffn, xb,
                                         ALU.mult, ALU.add).then_inc(out_done, 1)

            dve.memset(act_in[:, :], 0.0).then_inc(zeroed, 1)
            dve.memset(comb[:, :, :], 0.0).then_inc(zeroed, 1)
            x_stats(0)
            topk_rounds(0, 0, 1)
            x_stats(1)
            topk_rounds(0, 1, ROUNDS)
            adjacency(0)
            finish_x2(0)
            normalise(0)
            y_lo(0)
            dve.wait_ge(zeroed, 2)
            for s in range(NSLOT):
                g, m = s // SLOTS, s % SLOTS
                b = g + 1
                if m == 0:
                    route_first(g)
                    if b < NB:
                        topk_rounds(b, 0, 1)
                    route_second(g)
                    if b < NB:
                        topk_rounds(b, 1, 2)
                if b < NB:
                    if 1 <= m <= 4:
                        topk_rounds(b, 2 * m, 2 * m + 2)
                    if m == 5:
                        adjacency(b)
                    if m == 6:
                        finish_x2(b)
                    if m == 7:
                        normalise(b)
                    if m == 8:
                        y_lo(b)
                        if b + 1 < NB:
                            x_stats(b + 1)
                hidden(s)
                if m == 2 and g >= 1:
                    result(g - 1)
            result(NB - 1)

        @block.gpsimd
        def _(pool):
            def ln1_coefficients(b):
                v = ln1[:, b, :, :]
                n = 4 * b
                pool.wait_ge(mv1_done, 2 * (b + 1))
                pool.tensor_scalar(v[:, 0, :], mv1[:, b, :, 1], EPS, None, ALU.add).then_inc(ln1_step, 1)
                pool.wait_ge(ln1_step, n + 1)
                pool.tensor_tensor(v[:, 1, :], v[:, 0, :], half_col, ALU.pow).then_inc(ln1_step, 1)
                pool.wait_ge(ln1_step, n + 2)
                pool.tensor_scalar(v[:, 1, :], v[:, 1, :], c_res, None, ALU.mult).then_inc(ln1_step, 1)
                pool.wait_ge(ln1_step, n + 3)
                pool.tensor_scalar(v[:, 2, :], v[:, 1, :], 1.0, None, ALU.add)
                pool.tensor_tensor(v[:, 3, :], v[:, 1, :], mv1[:, b, :, 0], ALU.mult).then_inc(ln1_step, 1)
                pool.wait_ge(ln1_step, n + 4)
                pool.tensor_scalar(v[:, 3, :], v[:, 3, :], -1.0, None, ALU.mult).then_inc(ln1_done, 1)

            def one_plus_tanh(b):
                pool.wait_ge(tanh_done, b + 1)
                pool.tensor_scalar(th1[:, :, :], th1[:, :, :], 1.0, None, ALU.add).then_inc(th1_done, 1)

            def rstd2(b):
                pool.wait_ge(mv2_done, 2 * (b + 1))
                pool.tensor_scalar(rs2[:, 0, :], mv2[:, :, 1], EPS, None, ALU.add).then_inc(rs2_step, 1)
                pool.wait_ge(rs2_step, b + 1)
                pool.tensor_tensor(rs2[:, 1, :], rs2[:, 0, :], half_col, ALU.pow).then_inc(rs2_done, 1)

            def weights_lo(n):
                w = min(PIECE, WCOLS - n * PIECE)
                cols = slice(n * PIECE, n * PIECE + w)
                pool.wait_ge(whi_done, n + 1)
                pool.tensor_tensor(w_lo[:, cols], raw[:, n % RING, 0:w], w_hi[:, cols].bitcast(F32),
                                   ALU.subtract).then_inc(wlo_done, 1)

            def hidden_lo(s):
                rows, cols = (slice(0, P), 512) if s % SLOTS < PAIRS else (slice(P - TAIL, P), NTOK)
                pool.wait_ge(hhi_done, s + 1)
                if s % SLOTS == PAIRS:
                    pool.wait_ge(hlo_done, s)
                pool.tensor_tensor(h_lo[rows, s % 3, 0:cols], h32[rows, s % 2, 0:cols],
                                   h_hi[rows, s % 3, 0:cols].bitcast(F32), ALU.subtract).then_inc(hlo_done, 1)
                if s % SLOTS == PAIRS:
                    pool.wait_ge(hlo_done, s + 1)

            half_col = minus_half.to_broadcast([P, 2])
            pool.wait_ge(tscal_done, 2)
            pool.tensor_scalar(coef[:, 3:4], tscal[:, 2:3], 0.125, 0.125, ALU.mult, ALU.add).then_inc(coef_step, 1)
            pool.tensor_scalar(coef[:, 0:1], tscal[:, 2:3], -0.5, 0.5, ALU.mult, ALU.add).then_inc(coef_step, 1)
            pool.wait_ge(coef_step, 2)
            pool.tensor_tensor(coef[:, 2:3], coef[:, 3:4], tscal[:, 0:1], ALU.mult).then_inc(coef_step, 1)
            pool.tensor_tensor(coef[:, 1:2], coef[:, 0:1], tscal[:, 0:1], ALU.mult).then_inc(coef_step, 1)
            pool.wait_ge(coef_step, 4)
            pool.wait_ge(const_in, 16)
            ln1_coefficients(0)
            weights_lo(0)
            one_plus_tanh(0)
            pool.wait_ge(sel_in, 16)
            pool.tensor_copy(sel_r[:, :], sel_raw[:, :]).then_inc(consts_split, 1)
            pool.wait_ge(gw_in, 16)
            pool.tensor_copy(gw_hi[:, :], gw_raw[:, :]).then_inc(consts_split, 1)
            pool.wait_ge(consts_split, 2)
            pool.tensor_tensor(gw_lo[:, :], gw_raw[:, :], gw_hi[:, :].bitcast(F32), ALU.subtract).then_inc(consts_split, 1)
            ln1_coefficients(1)
            for n in range(1, EARLY):
                weights_lo(n)
                if n == EARLY - 2:
                    rstd2(0)
            one_plus_tanh(1)
            for s in range(NSLOT):
                g, m = s // SLOTS, s % SLOTS
                if g == 0 and EARLY + m < len(PIECES):
                    weights_lo(EARLY + m)
                if m == 1 and g >= 1 and g + 1 < NB:
                    ln1_coefficients(g + 1)
                if m == 6 and g + 1 < NB:
                    rstd2(g + 1)
                hidden_lo(s)
                if m == 6 and g + 2 < NB:
                    one_plus_tanh(g + 2)


_SHAPE = (NB, NTOK, D)


def kernel(x, ctx_512, g_xattn, g_ffn, L0_xattn_Wq, L0_xattn_Wk, L0_xattn_gamma_raw, L0_ffn_gate_w, L0_ffn_w_gate,
           L0_ffn_w_up, L0_ffn_w_down, L0_ffn_sw_gate, L0_ffn_sw_up, L0_ffn_sw_down, L0_ffn_shared_gate_w):
    import numpy as np
    import concourse.bacc as bacc
    from concourse.bass_utils import run_bass_kernel_spmd

    f = np.float32
    a = np.asarray
    gate = np.concatenate([a(L0_ffn_w_gate).transpose(1, 0, 2).reshape(D, E * EI), a(L0_ffn_sw_gate)], axis=1)
    up = np.concatenate([a(L0_ffn_w_up).transpose(1, 0, 2).reshape(D, E * EI), a(L0_ffn_sw_up)], axis=1)
    down = np.concatenate([a(L0_ffn_w_down).reshape(E * EI, D), a(L0_ffn_sw_down)], axis=0)
    whole = CHUNKS * P
    gu = np.stack([gate[:, :whole], up[:, :whole]]).reshape(2, KD, P, CHUNKS, P).transpose(2, 3, 0, 1, 4)
    wd = down[:whole].reshape(CHUNKS, P, D).transpose(1, 0, 2)
    wpack = np.zeros((P, WCOLS), f)
    for n, (kind, c) in enumerate(PIECES):
        at = n * PIECE
        if kind == "gu":
            wpack[:, at:at + PIECE] = gu[:, c:c + 2].reshape(P, PIECE)
        elif kind == "wd":
            wpack[:, at:at + PIECE] = wd[:, c:c + 4].reshape(P, PIECE)
        else:
            both = np.concatenate([gate[:, whole:], up[:, whole:]], axis=1)
            wpack[:, at:at + 256] = both.reshape(KD, P, P).transpose(1, 0, 2).reshape(P, KD * P)
            wpack[P - TAIL:, at + 256:at + 512] = down[whole:]
    gw = np.zeros((P, KD, CW), f)
    gw[:, :, 0:E] = a(L0_ffn_gate_w).T.reshape(KD, P, E).transpose(1, 0, 2)
    gw[:, :, E] = a(L0_ffn_shared_gate_w).reshape(KD, P).T
    const = np.zeros((P, P + 9), f)
    const[:, 0:P] = np.eye(P, dtype=f)
    const[:, P:P + 8] = np.arange(8, dtype=f)
    const[:, P + 8] = -0.5
    owner = np.concatenate([np.arange(E * EI) // EI, np.full(P, E)])
    sel = np.zeros((2, CW, NSEL * P), f)
    sel[:, owner, np.arange(NSEL * P)] = 1
    arrays = {
        "x": np.ascontiguousarray(x),
        "ctx_t": np.ascontiguousarray(a(ctx_512).transpose(2, 0, 1).reshape(DC, NB * NTOK)),
        "wqk": np.ascontiguousarray(np.concatenate([a(L0_xattn_Wq), a(L0_xattn_Wk)], axis=1)),
        "scal": np.ascontiguousarray(np.tile(np.array([a(g_xattn).reshape(-1)[0], a(g_ffn).reshape(-1)[0],
                                                       a(L0_xattn_gamma_raw).reshape(-1)[0]], f), (P, 1))),
        "gw": gw.reshape(P, KD * CW),
        "sel": sel.reshape(2 * CW, NSEL * P),
        "const": const,
        "wpack": wpack,
    }
    nc = bacc.Bacc("TRN2", target_bir_lowering=False, num_devices=1)
    aps = [nc.dram_tensor(n, v.shape, mybir.dt.from_np(v.dtype), kind="ExternalInput").ap() for n, v in arrays.items()]
    out = nc.dram_tensor("out", _SHAPE, F32, kind="ExternalOutput").ap()
    build(nc, *aps, out)
    r = run_bass_kernel_spmd(nc, [arrays], core_ids=[0])
    return r.results[0]["out"]
```

```python
from contextlib import ExitStack

import concourse.bass as bass
from concourse import mybir

ALU = mybir.AluOpType
ACT = mybir.ActivationFunctionType
F32 = mybir.dt.float32
F32R = mybir.dt.float32r
U32 = mybir.dt.uint32

P = 128
NB, NTOK, D, DC = 4, 256, 256, 64
KD = D // P
E, EI, SI = 8, 176, 704
MOE_CH = E * EI // P
CHUNKS = (E * EI + SI) // P
TAIL = E * EI + SI - CHUNKS * P
PAIRS = CHUNKS // 2
SLOTS = PAIRS + 1
TOPK = int(NTOK * 0.3)
ROUNDS = (TOPK + 7) // 8
EPS = 1e-5
CW = 10
CB_WRITES = (MOE_CH + 1) // 2
BIG = 3.0e38
assert 2 * PAIRS == CHUNKS and TAIL == 64 and NTOK == 2 * P

PIECE = 1024
PIECES = []
for _q in range(CHUNKS // 4):
    PIECES += [("gu", 4 * _q), ("gu", 4 * _q + 2), ("wd", 4 * _q)]
PIECES += [("tail", CHUNKS)]
C_IOTA, C_HALF, C_SCAL, C_GW = P, P + 8, P + 9, P + 12
CONST = C_GW + KD * CW
WCOLS = PIECE * (len(PIECES) - 1) + 512
RING = 5
WARM = 8
EARLY = 7


def gu_at(chunk):
    n = PIECES.index(("tail", CHUNKS) if chunk == CHUNKS else ("gu", chunk - chunk % 2))
    return n, n * PIECE + (0 if chunk == CHUNKS else 512 * (chunk % 2))


def wd_at(chunk):
    n = PIECES.index(("tail", CHUNKS) if chunk == CHUNKS else ("wd", chunk - chunk % 4))
    return n, n * PIECE + (256 if chunk == CHUNKS else 256 * (chunk % 4))


def build(nc, x, qk_in, sel, const, wpack, out):
    x_v = x.rearrange("b (r p) d -> p (b r) d", p=P)
    out_v = out.rearrange("b (r p) d -> p (b r) d", p=P)
    NSLOT = NB * SLOTS

    with ExitStack() as ctx:
        def sb(name, shape, dt=F32):
            return ctx.enter_context(nc.sbuf_tensor(name, shape, dt))

        def sem(name):
            return ctx.enter_context(nc.semaphore(name))

        def bank(name):
            return ctx.enter_context(nc.psum_tensor(name, [P, 512], F32))

        gate_ps = [bank("gate0"), bank("gate1")]
        up_ps = [bank("up0"), bank("up1")]
        cb_ps = bank("cb")
        down_ps = [bank("down0"), bank("down1")]
        misc_ps = bank("misc")

        xs = sb("xs", [P, 2 * NB, D])
        qk_sb = sb("qk_sb", [DC, 2 * DC + NB * NTOK])
        w_qk = qk_sb[:, 0:2 * DC]
        ctxT = qk_sb[:, 2 * DC:]
        qT = sb("qT", [DC, NB * NTOK])
        kT = sb("kT", [DC, NB * NTOK])
        const_sb = sb("const_sb", [P, CONST])
        ident = const_sb[:, 0:P]
        iota8 = const_sb[:, C_IOTA:C_IOTA + 8]
        minus_half = const_sb[:, C_HALF:C_HALF + 1]
        scal_sb = const_sb[:, C_SCAL:C_SCAL + 3]
        gw_raw = const_sb[:, C_GW:C_GW + KD * CW]
        idle = sb("idle", [P, 512], mybir.dt.bfloat16)
        tscal = sb("tscal", [P, 3])
        coef = sb("coef", [P, 4])
        c_res, c_adj, c_ffn = coef[:, 1:2], coef[:, 2:3], tscal[:, 1:2]
        gw_hi = sb("gw_hi", [P, KD * CW], F32R)
        gw_lo = sb("gw_lo", [P, KD * CW], F32R)
        sel_raw = sb("sel_raw", [2 * CW, MOE_CH * P])
        sel_r = sb("sel_r", [2 * CW, MOE_CH * P], F32R)
        shared_w = sb("shared_w", [P, NB, 2])
        raw = sb("raw", [P, RING, PIECE])
        w_hi = sb("w_hi", [P, WCOLS], F32R)
        w_lo = sb("w_lo", [P, WCOLS], F32R)
        sim = sb("sim", [P, 2, NTOK])
        work = sb("work", [P, 2, NTOK])
        top8 = sb("top8", [P, 2, 8])
        th1 = sb("th1", [P, 2, NTOK])
        adj = sb("adj", [P, 2, NTOK])
        st1 = sb("st1", [P, 2, 6])
        mv1 = sb("mv1", [P, NB, 2, 2])
        ln1 = sb("ln1", [P, NB, 4, 2])
        st2 = sb("st2", [P, 2, 6])
        mv2 = sb("mv2", [P, 2, 2])
        rs2 = sb("rs2", [P, 2, 2])
        y = sb("y", [P, 2, D])
        yT_hi = sb("yT_hi", [P, NB, 2 * NTOK], F32R)
        yT_lo = sb("yT_lo", [P, NB, 2 * NTOK], F32R)
        lg = sb("lg", [P, 2, CW])
        lmax = sb("lmax", [P, 2, 8])
        lidx = sb("lidx", [P, 2, 8], U32)
        lidf = sb("lidf", [P, 2, 8])
        dz = sb("dz", [P, 2, 2])
        tdz = sb("tdz", [P, 2, 2])
        wts = sb("wts", [P, 2, 3])
        pick = sb("pick", [P, 2, 8])
        comb = sb("comb", [P, 2, CW])
        comb_split = sb("comb_split", [P, 2, 2 * CW])
        cT = sb("cT", [2 * CW, NB * NTOK], F32R)
        act_in = sb("act_in", [P, 1])
        act_out = sb("act_out", [P, 1])
        silu_sb = sb("silu_sb", [P, 2, 512])
        h32 = sb("h32", [P, 2, 512])
        h_hi = sb("h_hi", [P, 3, 512], F32R)
        h_lo = sb("h_lo", [P, 3, 512], F32R)
        comb_hi = sb("comb_hi", [P, 2, CW], F32R)

        qk0_in, ctx_in, sel_in, const_in = (sem(n) for n in ("qk0_in", "ctx_in", "sel_in", "const_in"))
        x_in = [sem(f"x_in{b}") for b in range(NB)]
        raw_in = [sem(f"raw_in{s}") for s in range(RING)]
        out_sent = sem("out_sent")
        qk_ready, sim_ready, adjT_ready, yT_ready, logit_ready, cT_ready = (sem(n) for n in (
            "qk_ready", "sim_ready", "adjT_ready", "yT_ready", "logit_ready", "cT_ready"))
        gu_ready, cb_ready, down_done = sem("gu_ready"), sem("cb_ready"), sem("down_done")
        tscal_done, q_copied, sim_copied, tanh_done, th1_done, base_done, sel_done = (sem(n) for n in (
            "tscal_done", "q_copied", "sim_copied", "tanh_done", "th1_done", "base_done", "sel_done"))
        yhi_done, tdz_done, cT_copied, silu_done, hhi_done, whi_done = (sem(n) for n in (
            "yhi_done", "tdz_done", "cT_copied", "silu_done", "hhi_done", "whi_done"))
        zeroed, xstat_step, mv1_done, topk_step, adj_done, x2a_done, x2_done = (sem(n) for n in (
            "zeroed", "xstat_step", "mv1_done", "topk_step", "adj_done", "x2a_done", "x2_done"))
        stat2_step, mv2_done, y_done, ylo_done, route_step, dz_done, comb_done = (sem(n) for n in (
            "stat2_step", "mv2_done", "y_done", "ylo_done", "route_step", "dz_done", "comb_done"))
        t2_done, hid_done, moe_added, out_done, k_copied, shared_done = (sem(n) for n in (
            "t2_done", "hid_done", "moe_added", "out_done", "k_copied", "shared_done"))
        gw_split, coef_step, ln1_step, ln1_done = (sem(n) for n in (
            "gw_split", "coef_step", "ln1_step", "ln1_done"))
        rs2_step, rs2_done, wlo_done, hlo_done = (sem(n) for n in (
            "rs2_step", "rs2_done", "wlo_done", "hlo_done"))

        def sim_bank(b, r):
            return down_ps[1][:, 0:NTOK] if b == 0 and r == 1 else misc_ps[:, r * NTOK:(r + 1) * NTOK]

        def qk_bank(b):
            return (up_ps[1], gate_ps[0], gate_ps[1], up_ps[0])[b]

        def hidden_made(eng, s):
            if s % SLOTS < CB_WRITES:
                eng.wait_ge(hid_done, s // SLOTS * CB_WRITES + s % SLOTS + 1)
            else:
                eng.wait_ge(t2_done, s + 1)

        block = ctx.enter_context(nc.Block())

        @block.sync
        def _(sp):
            first = 2 * DC + NTOK
            sp.dma_start(qk_sb[:, 0:first], qk_in[:, 0:first]).then_inc(qk0_in, 16)
            for n in range(len(PIECES)):
                if n >= RING:
                    sp.wait_ge(wlo_done, n - RING + 1)
                w = min(PIECE, WCOLS - n * PIECE)
                sp.dma_start(raw[:, n % RING, 0:w], wpack[:, n * PIECE:n * PIECE + w]).then_inc(raw_in[n % RING], 16)
                if n == 0:
                    sp.dma_start(qk_sb[:, first:], qk_in[:, first:]).then_inc(ctx_in, 16)
                if n < NB:
                    b = n
                    sp.dma_start(xs[:, 2 * b:2 * b + 2, :], x_v[:, 2 * b:2 * b + 2, :]).then_inc(x_in[b], 16)
            for i in range(2 * NB):
                sp.wait_ge(out_done, i + 1)
                sp.dma_start(out_v[:, i, :], xs[:, i, :]).then_inc(out_sent, 16)
            sp.wait_ge(out_sent, 16 * 2 * NB)

        @block.tensor
        def _(pe):
            def query_key(b, ps):
                pe.matmul(ps[:, 0:NTOK], w_qk, ctxT[:, b * NTOK:(b + 1) * NTOK],
                          start=True, stop=True).then_inc(qk_ready, 1)

            def similarity(b):
                pe.wait_ge(q_copied, b + 1)
                pe.wait_ge(k_copied, b + 1)
                for r in range(2):
                    i = 2 * b + r
                    pe.matmul(sim_bank(b, r), qT[:, i * P:(i + 1) * P], kT[:, b * NTOK:(b + 1) * NTOK],
                              start=True, stop=True).then_inc(sim_ready, 1)

            def transpose_adj(b):
                pe.wait_ge(adj_done, 2 * (b + 1))
                for r in range(2):
                    for c in range(2):
                        last = pe.transpose(misc_ps[:, r * NTOK + c * P:r * NTOK + (c + 1) * P],
                                            adj[:, c, r * P:(r + 1) * P], ident)
                last.then_inc(adjT_ready, 1)

            def transpose_y(b):
                pe.wait_ge(y_done, 2 * (b + 1))
                for k in range(KD):
                    for r in range(2):
                        last = pe.transpose(misc_ps[:, k * NTOK + r * P:k * NTOK + (r + 1) * P],
                                            y[:, r, k * P:(k + 1) * P], ident)
                last.then_inc(yT_ready, 1)

            def logits(b):
                pe.wait_ge(yhi_done, b + 1)
                pe.wait_ge(ylo_done, b + 1)
                pe.wait_ge(gw_split, 2)
                for r in range(2):
                    for k in range(KD):
                        at = slice(k * NTOK + r * P, k * NTOK + (r + 1) * P)
                        gk = slice(k * CW, (k + 1) * CW)
                        for n, (a, w) in enumerate(((yT_hi, gw_hi), (yT_hi, gw_lo), (yT_lo, gw_hi))):
                            last = pe.matmul(misc_ps[:, r * CW:(r + 1) * CW], a[:, b, at], w[:, gk],
                                             start=(k == 0 and n == 0), stop=(k == KD - 1 and n == 2))
                last.then_inc(logit_ready, 1)

            def transpose_comb(b):
                pe.wait_ge(comb_done, b + 1)
                for r in range(2):
                    last = pe.transpose(misc_ps[0:2 * CW, r * P:(r + 1) * P], comb_split[:, r, :], ident)
                last.then_inc(cT_ready, 1)

            def gate_up(s):
                g, m = s // SLOTS, s % SLOTS
                if m == 0:
                    pe.wait_ge(yhi_done, g + 1)
                    pe.wait_ge(ylo_done, g + 1)
                if s >= 2:
                    pe.wait_ge(silu_done, s - 1)
                    pe.wait_ge(t2_done, s - 1)
                chunks = (2 * m, 2 * m + 1) if m < PAIRS else (CHUNKS,)
                for q, c in enumerate(chunks):
                    n, col = gu_at(c)
                    if g == 0:
                        pe.wait_ge(whi_done, n + 1)
                        pe.wait_ge(wlo_done, n + 1)
                    for half, dst in enumerate((gate_ps, up_ps) if m < PAIRS else (gate_ps,)):
                        for k in range(KD):
                            wk = slice(col + (half * KD + k) * P, col + (half * KD + k + 1) * P)
                            yk = slice(k * NTOK, (k + 1) * NTOK)
                            for t, (w, a) in enumerate(((w_hi, yT_hi), (w_hi, yT_lo), (w_lo, yT_hi))):
                                last = pe.matmul(dst[s % 2][:, q * NTOK:(q + 1) * NTOK], w[:, wk], a[:, g, yk],
                                                 start=(k == 0 and t == 0), stop=(k == KD - 1 and t == 2))
                last.then_inc(gu_ready, 1)

            def spread_c(s):
                g, m = s // SLOTS, s % SLOTS
                if m >= CB_WRITES:
                    return
                if m == 0:
                    pe.wait_ge(cT_copied, g + 1)
                    pe.wait_ge(sel_done, 1)
                if s >= 1:
                    pe.wait_ge(hid_done, g * CB_WRITES + m)
                for j in range(2 * m, min(2 * m + 2, MOE_CH)):
                    q = j % 2
                    last = pe.matmul(cb_ps[:, q * NTOK:(q + 1) * NTOK], sel_r[:, j * P:(j + 1) * P],
                                     cT[:, g * NTOK:(g + 1) * NTOK], start=True, stop=True)
                last.then_inc(cb_ready, 1)

            def down(s):
                g, m = s // SLOTS, s % SLOTS
                pe.wait_ge(hhi_done, s + 1)
                pe.wait_ge(hlo_done, s + 1)
                if m == 0 and g >= 1:
                    pe.wait_ge(moe_added, g)
                if m == MOE_CH // 2 and g >= 1:
                    pe.wait_ge(out_done, 2 * g)
                chunks = (2 * m, 2 * m + 1) if m < PAIRS else (CHUNKS,)
                for q, c in enumerate(chunks):
                    n, col = wd_at(c)
                    if g == 0:
                        pe.wait_ge(whi_done, n + 1)
                        pe.wait_ge(wlo_done, n + 1)
                    rows = slice(0, P) if c < CHUNKS else slice(P - TAIL, P)
                    wc = slice(col, col + D)
                    for r in range(2):
                        at = slice(q * NTOK + r * P, q * NTOK + (r + 1) * P)
                        for t, (h, w) in enumerate(((h_hi, w_hi), (h_hi, w_lo), (h_lo, w_hi))):
                            last = pe.matmul(down_ps[c >= MOE_CH][:, r * D:(r + 1) * D], h[rows, s % 3, at], w[rows, wc],
                                             start=(c in (0, MOE_CH) and r == 0 and t == 0),
                                             stop=(c in (MOE_CH - 1, CHUNKS) and t == 2),
                                             skip_group_check=True)
                last.then_inc(down_done, 1)

            pe.wait_ge(zeroed, 1)
            for _ in range(WARM):
                pe.matmul(gate_ps[0][:, :], idle[:, 0:P], idle[:, :], start=True, stop=True)
            pe.wait_ge(qk0_in, 16)
            query_key(0, qk_bank(0))
            similarity(0)
            pe.wait_ge(const_in, 16)
            transpose_adj(0)
            pe.wait_ge(ctx_in, 16)
            for b in range(1, NB):
                query_key(b, qk_bank(b))
            pe.wait_ge(x2_done, 1)
            similarity(1)
            pe.wait_ge(sim_copied, 4)
            transpose_y(0)
            logits(0)
            pe.wait_ge(q_copied, NB)
            pe.wait_ge(k_copied, NB)
            for s in range(NSLOT):
                g, m = s // SLOTS, s % SLOTS
                gate_up(s)
                if m == 0:
                    transpose_comb(g)
                if m == 5 and g + 1 < NB:
                    pe.wait_ge(cT_copied, g + 1)
                    transpose_adj(g + 1)
                if m == 6 and g + 2 < NB:
                    pe.wait_ge(x2_done, g + 2)
                    similarity(g + 2)
                if m == 7 and g + 1 < NB:
                    if g + 2 < NB:
                        pe.wait_ge(sim_copied, 2 * (g + 3))
                    transpose_y(g + 1)
                if m == 8 and g + 1 < NB:
                    logits(g + 1)
                if s >= 2:
                    down(s - 2)
                spread_c(s)
            down(NSLOT - 2)
            down(NSLOT - 1)

        @block.scalar
        def _(act):
            def weights_hi(n):
                w = min(PIECE, WCOLS - n * PIECE)
                act.wait_ge(raw_in[n % RING], 16 * (n // RING + 1))
                act.activation(w_hi[:, n * PIECE:n * PIECE + w], raw[:, n % RING, 0:w], ACT.Copy).then_inc(whi_done, 1)

            def copy_q(b):
                act.wait_ge(qk_ready, b + 1)
                act.activation(qT[:, b * NTOK:(b + 1) * NTOK], qk_bank(b)[0:DC, 0:NTOK], ACT.Copy).then_inc(q_copied, 1)

            def copy_k(b):
                act.activation(kT[:, b * NTOK:(b + 1) * NTOK], qk_bank(b)[DC:2 * DC, 0:NTOK], ACT.Copy).then_inc(k_copied, 1)

            def copy_sim(b):
                if b >= 1:
                    act.wait_ge(adj_done, 2 * b)
                for r in range(2):
                    act.wait_ge(sim_ready, 2 * b + (r + 1 if b == 0 else 2))
                    act.activation(sim[:, r, :], sim_bank(b, r), ACT.Copy).then_inc(sim_copied, 1)
                act.wait_ge(sim_copied, 2 * b + 2)
                act.activation(th1[:, :, :], sim[:, :, :], ACT.Tanh, scale=1.0 / 32).then_inc(tanh_done, 1)
                act.wait_ge(tanh_done, b + 1)
                act.activation(th1[:, :, :], th1[:, :, :], ACT.Copy, bias=1.0).then_inc(th1_done, 1)

            def residual_base(b):
                act.wait_ge(ln1_done, b + 1)
                for r in range(2):
                    act.activation(xs[:, 2 * b + r, :], xs[:, 2 * b + r, :], ACT.Identity,
                                   bias=ln1[:, b, 3, r:r + 1], scale=ln1[:, b, 2, r:r + 1]).then_inc(base_done, 1)

            def split_y(b):
                act.wait_ge(yT_ready, b + 1)
                act.activation(yT_hi[:, b, :], misc_ps[:, :], ACT.Copy).then_inc(yhi_done, 1)

            def silu(s):
                act.wait_ge(gu_ready, s + 1)
                if s >= 2:
                    act.wait_ge(t2_done, s - 1)
                if s % SLOTS < PAIRS:
                    act.activation(silu_sb[:, s % 2, :], gate_ps[s % 2][:, :], ACT.Silu).then_inc(silu_done, 1)
                else:
                    act.activation(silu_sb[P - TAIL:P, s % 2, 0:NTOK], gate_ps[s % 2][0:TAIL, 0:NTOK],
                                   ACT.Silu).then_inc(silu_done, 1)

            def hidden_hi(s):
                hidden_made(act, s)
                if s >= 3:
                    act.wait_ge(down_done, s - 2)
                rows, cols = (slice(0, P), 512) if s % SLOTS < PAIRS else (slice(P - TAIL, P), NTOK)
                act.activation(h_hi[rows, s % 3, 0:cols], h32[rows, s % 2, 0:cols], ACT.Copy).then_inc(hhi_done, 1)

            act.wait_ge(zeroed, 2)
            act.activation(act_out[:, :], act_in[:, :], ACT.Silu)
            copy_q(0)
            copy_sim(0)
            act.wait_ge(const_in, 16)
            act.activation(tscal[:, 0:2], scal_sb[:, 0:2], ACT.Tanh).then_inc(tscal_done, 1)
            act.activation(tscal[:, 2:3], scal_sb[:, 2:3], ACT.Tanh, scale=0.5).then_inc(tscal_done, 1)
            for n in range(EARLY):
                weights_hi(n)
                if n == 2:
                    residual_base(0)
                if n == 4:
                    act.wait_ge(sel_in, 16)
                    act.activation(sel_r[:, :], sel_raw[:, :], ACT.Copy).then_inc(sel_done, 1)
            for b in range(1, NB):
                copy_q(b)
                copy_k(b)
            copy_sim(1)
            split_y(0)
            residual_base(1)
            for s in range(NSLOT):
                g, m = s // SLOTS, s % SLOTS
                if m == 0:
                    act.wait_ge(dz_done, g + 1)
                    act.activation(tdz[:, :, :], dz[:, :, :], ACT.Tanh, scale=0.5).then_inc(tdz_done, 1)
                silu(s)
                if m == 0:
                    act.wait_ge(cT_ready, g + 1)
                    act.activation(cT[:, g * NTOK:(g + 1) * NTOK], misc_ps[0:2 * CW, 0:NTOK], ACT.Copy).then_inc(cT_copied, 1)
                if g == 0 and EARLY + m < len(PIECES):
                    weights_hi(EARLY + m)
                if m == 3 and g >= 1 and g + 1 < NB:
                    residual_base(g + 1)
                if m == 6 and g + 2 < NB:
                    copy_sim(g + 2)
                if m == 7 and g + 1 < NB:
                    split_y(g + 1)
                hidden_hi(s)

        @block.vector
        def _(dve):
            def stats(tile, st, mv, step, done, count):
                for r in range(2):
                    dve.bn_stats(st[:, r, :], tile[:, r, :]).then_inc(step, 1)
                for r in range(2):
                    dve.wait_ge(step, 2 * count + r + 1)
                    dve.bn_aggr(mv[:, r, :], st[:, r, :]).then_inc(done, 1)

            def x_stats(b):
                dve.wait_ge(x_in[b], 16)
                if b >= 1:
                    dve.wait_ge(mv1_done, 2 * b)
                stats(xs[:, 2 * b:2 * b + 2, :], st1, mv1[:, b, :, :], xstat_step, mv1_done, b)

            def topk_rounds(b, first, end):
                def follow(n):
                    if n >= 2:
                        dve.wait_ge(topk_step, n - 1)

                for k in range(first, end):
                    n = b * (4 * ROUNDS - 2) + 4 * k
                    for r in range(2):
                        if k == 0:
                            dve.wait_ge(sim_copied, 2 * b + r + 1)
                        follow(n + r)
                        dve.max(top8[:, r, :], (sim if k == 0 else work)[:, r, :]).then_inc(topk_step, 1)
                    if k < ROUNDS - 1:
                        for r in range(2):
                            follow(n + 2 + r)
                            dve.match_replace(work[:, r, :], top8[:, r, :], (sim if k == 0 else work)[:, r, :],
                                              -BIG).then_inc(topk_step, 1)

            def adjacency(b):
                kth = TOPK - 8 * (ROUNDS - 1) - 1
                dve.wait_ge(th1_done, b + 1)
                if b >= 1:
                    dve.wait_ge(adjT_ready, b)
                for r in range(2):
                    dve.wait_ge(topk_step, (b + 1) * (4 * ROUNDS - 2) - 1 + r)
                    dve.scalar_tensor_tensor(adj[:, r, :], sim[:, r, :], top8[:, r, kth:kth + 1], th1[:, r, :],
                                             ALU.is_ge, ALU.mult).then_inc(adj_done, 1)
                dve.wait_ge(adj_done, 2 * (b + 1))
                dve.wait_ge(base_done, 2 * (b + 1))
                xb = xs[:, 2 * b:2 * b + 2, :]
                dve.scalar_tensor_tensor(xb, adj[:, :, :], c_adj, xb, ALU.mult, ALU.add).then_inc(x2a_done, 1)

            def finish_x2(b):
                xb = xs[:, 2 * b:2 * b + 2, :]
                dve.wait_ge(x2a_done, b + 1)
                dve.wait_ge(adjT_ready, b + 1)
                dve.scalar_tensor_tensor(xb, misc_ps[:, :].rearrange("p (r n) -> p r n", r=2), c_adj, xb,
                                         ALU.mult, ALU.add).then_inc(x2_done, 1)
                dve.wait_ge(x2_done, b + 1)
                stats(xb, st2, mv2, stat2_step, mv2_done, b)

            def normalise(b):
                dve.wait_ge(rs2_done, b + 1)
                if b >= 1:
                    dve.wait_ge(yT_ready, b)
                for r in range(2):
                    dve.tensor_scalar(y[:, r, :], xs[:, 2 * b + r, :], mv2[:, r, 0:1], rs2[:, 1, r:r + 1],
                                      ALU.subtract, ALU.mult).then_inc(y_done, 1)

            def y_lo(b):
                dve.wait_ge(yhi_done, b + 1)
                dve.tensor_tensor(yT_lo[:, b, :], misc_ps[:, :], yT_hi[:, b, :].bitcast(F32),
                                  ALU.subtract).then_inc(ylo_done, 1)

            ROUTE = 15

            def route_first(b):
                n = b * ROUTE
                dve.wait_ge(logit_ready, b + 1)
                dve.tensor_copy(lg[:, :, :], misc_ps[:, 0:2 * CW].rearrange("p (r e) -> p r e", r=2)).then_inc(route_step, 1)
                dve.wait_ge(route_step, n + 1)
                for r in range(2):
                    dve.max(lmax[:, r, :], lg[:, r, 0:E]).then_inc(route_step, 1)
                dve.wait_ge(route_step, n + 3)
                dve.tensor_tensor(dz[:, :, 0:1], lmax[:, :, 0:1], lmax[:, :, 1:2], ALU.subtract).then_inc(route_step, 1)
                dve.wait_ge(route_step, n + 4)
                dve.tensor_copy(dz[:, :, 1:2], lg[:, :, E:E + 1]).then_inc(dz_done, 1)
                for r in range(2):
                    dve.max_index(lidx[:, r, :], lmax[:, r, :], lg[:, r, 0:E]).then_inc(route_step, 1)
                dve.wait_ge(route_step, n + 6)
                dve.tensor_copy(lidf[:, :, :], lidx[:, :, :]).then_inc(route_step, 1)

            def route_second(b):
                n = b * ROUTE + 7
                dve.wait_ge(tdz_done, b + 1)
                dve.tensor_scalar(wts[:, :, 0:2], tdz[:, :, :], 0.5, 0.5, ALU.mult, ALU.add).then_inc(route_step, 1)
                dve.tensor_scalar(wts[:, :, 2:3], tdz[:, :, 0:1], -0.5, 0.5, ALU.mult, ALU.add).then_inc(route_step, 1)
                dve.wait_ge(route_step, n + 2)
                for r in range(2):
                    dve.tensor_scalar(pick[:, r, :], iota8, lidf[:, r, 0:1], wts[:, r, 0:1],
                                      ALU.is_equal, ALU.mult).then_inc(route_step, 1)
                    dve.tensor_scalar(comb[:, r, 0:E], iota8, lidf[:, r, 1:2], wts[:, r, 2:3],
                                      ALU.is_equal, ALU.mult).then_inc(route_step, 1)
                dve.tensor_scalar(shared_w[:, b, :], wts[:, :, 1], c_ffn, None, ALU.mult).then_inc(shared_done, 1)
                dve.wait_ge(route_step, n + 6)
                dve.tensor_tensor(comb[:, :, 0:E], comb[:, :, 0:E], pick[:, :, :], ALU.add).then_inc(route_step, 1)
                dve.wait_ge(route_step, n + 7)
                dve.tensor_copy(comb_hi[:, :, :], comb[:, :, :]).then_inc(route_step, 1)
                dve.wait_ge(route_step, n + 8)
                if b >= 1:
                    dve.wait_ge(cT_ready, b)
                dve.tensor_copy(comb_split[:, :, 0:CW], comb_hi[:, :, :].bitcast(F32))
                dve.tensor_tensor(comb_split[:, :, CW:2 * CW], comb[:, :, :], comb_hi[:, :, :].bitcast(F32),
                                  ALU.subtract).then_inc(comb_done, 1)

            def hidden(s):
                g, m = s // SLOTS, s % SLOTS
                rows, cols, up = (slice(0, P), 512, up_ps) if m < PAIRS else (slice(P - TAIL, P), NTOK, gate_ps)
                dve.wait_ge(silu_done, s + 1)
                if s >= 2:
                    dve.wait_ge(hlo_done, s - 1)
                h = h32[rows, s % 2, 0:cols]
                dve.tensor_tensor(h, silu_sb[rows, s % 2, 0:cols], up[s % 2][rows, 0:cols], ALU.mult).then_inc(t2_done, 1)
                if m >= CB_WRITES:
                    return
                dve.wait_ge(t2_done, s + 1)
                dve.wait_ge(cb_ready, g * CB_WRITES + m + 1)
                moe = h32[:, s % 2, 0:NTOK * min(2, MOE_CH - 2 * m)]
                dve.tensor_tensor(moe, moe, cb_ps[:, 0:moe.shape[1]], ALU.mult).then_inc(hid_done, 1)

            def add_moe(b):
                xb = xs[:, 2 * b:2 * b + 2, :]
                dve.wait_ge(down_done, SLOTS * b + MOE_CH // 2 + 1)
                dve.scalar_tensor_tensor(xb, down_ps[0][:, :].rearrange("p (r n) -> p r n", r=2), c_ffn, xb,
                                         ALU.mult, ALU.add).then_inc(moe_added, 1)

            def add_shared(b):
                dve.wait_ge(moe_added, b + 1)
                dve.wait_ge(shared_done, b + 1)
                dve.wait_ge(down_done, SLOTS * (b + 1))
                for r in range(2):
                    xr = xs[:, 2 * b + r, :]
                    dve.scalar_tensor_tensor(xr, down_ps[1][:, r * D:(r + 1) * D], shared_w[:, b, r:r + 1], xr,
                                             ALU.mult, ALU.add).then_inc(out_done, 1)

            dve.memset(idle[:, :], 0.0).then_inc(zeroed, 1)
            dve.memset(act_in[:, :], 0.0).then_inc(zeroed, 1)
            dve.memset(comb[:, :, :], 0.0).then_inc(zeroed, 1)
            dve.wait_ge(qk_ready, 1)
            dve.tensor_copy(kT[:, 0:NTOK], qk_bank(0)[DC:2 * DC, 0:NTOK]).then_inc(k_copied, 1)
            x_stats(0)
            topk_rounds(0, 0, ROUNDS)
            adjacency(0)
            finish_x2(0)
            normalise(0)
            y_lo(0)
            x_stats(1)
            dve.wait_ge(zeroed, 3)
            for s in range(NSLOT):
                g, m = s // SLOTS, s % SLOTS
                b = g + 1
                if m == 0:
                    route_first(g)
                    if b < NB:
                        topk_rounds(b, 0, 1)
                    route_second(g)
                    if b < NB:
                        topk_rounds(b, 1, 2)
                if b < NB:
                    if 1 <= m <= 4:
                        topk_rounds(b, 2 * m, 2 * m + 2)
                    if m == 5:
                        adjacency(b)
                    if m == 6:
                        finish_x2(b)
                    if m == 7:
                        normalise(b)
                    if m == 8:
                        y_lo(b)
                        if b + 1 < NB:
                            x_stats(b + 1)
                hidden(s)
                if m == 2 and g >= 1:
                    add_shared(g - 1)
                if m == SLOTS - 1:
                    add_moe(g)
            add_shared(NB - 1)

        @block.gpsimd
        def _(pool):
            def ln1_coefficients(b):
                v = ln1[:, b, :, :]
                n = 4 * b
                pool.wait_ge(mv1_done, 2 * (b + 1))
                pool.tensor_scalar(v[:, 0, :], mv1[:, b, :, 1], EPS, None, ALU.add).then_inc(ln1_step, 1)
                pool.wait_ge(ln1_step, n + 1)
                pool.tensor_tensor(v[:, 1, :], v[:, 0, :], half_col, ALU.pow).then_inc(ln1_step, 1)
                pool.wait_ge(ln1_step, n + 2)
                pool.tensor_scalar(v[:, 1, :], v[:, 1, :], c_res, None, ALU.mult).then_inc(ln1_step, 1)
                pool.wait_ge(ln1_step, n + 3)
                pool.tensor_scalar(v[:, 2, :], v[:, 1, :], 1.0, None, ALU.add)
                pool.tensor_tensor(v[:, 3, :], v[:, 1, :], mv1[:, b, :, 0], ALU.mult).then_inc(ln1_step, 1)
                pool.wait_ge(ln1_step, n + 4)
                pool.tensor_scalar(v[:, 3, :], v[:, 3, :], -1.0, None, ALU.mult).then_inc(ln1_done, 1)

            def rstd2(b):
                pool.wait_ge(mv2_done, 2 * (b + 1))
                pool.tensor_scalar(rs2[:, 0, :], mv2[:, :, 1], EPS, None, ALU.add).then_inc(rs2_step, 1)
                pool.wait_ge(rs2_step, b + 1)
                pool.tensor_tensor(rs2[:, 1, :], rs2[:, 0, :], half_col, ALU.pow).then_inc(rs2_done, 1)

            def weights_lo(n):
                w = min(PIECE, WCOLS - n * PIECE)
                cols = slice(n * PIECE, n * PIECE + w)
                pool.wait_ge(whi_done, n + 1)
                pool.tensor_tensor(w_lo[:, cols], raw[:, n % RING, 0:w], w_hi[:, cols].bitcast(F32),
                                   ALU.subtract).then_inc(wlo_done, 1)

            def hidden_lo(s):
                rows, cols = (slice(0, P), 512) if s % SLOTS < PAIRS else (slice(P - TAIL, P), NTOK)
                pool.wait_ge(hhi_done, s + 1)
                if s % SLOTS == PAIRS:
                    pool.wait_ge(hlo_done, s)
                pool.tensor_tensor(h_lo[rows, s % 3, 0:cols], h32[rows, s % 2, 0:cols],
                                   h_hi[rows, s % 3, 0:cols].bitcast(F32), ALU.subtract).then_inc(hlo_done, 1)
                if s % SLOTS == PAIRS:
                    pool.wait_ge(hlo_done, s + 1)

            half_col = minus_half.to_broadcast([P, 2])
            pool.dma_start(const_sb[:, :], const).then_inc(const_in, 16)
            pool.dma_start(sel_raw[:, :], sel).then_inc(sel_in, 16)
            pool.wait_ge(tscal_done, 2)
            pool.tensor_scalar(coef[:, 3:4], tscal[:, 2:3], 0.125, 0.125, ALU.mult, ALU.add).then_inc(coef_step, 1)
            pool.tensor_scalar(coef[:, 0:1], tscal[:, 2:3], -0.5, 0.5, ALU.mult, ALU.add).then_inc(coef_step, 1)
            pool.wait_ge(coef_step, 2)
            pool.tensor_tensor(coef[:, 2:3], coef[:, 3:4], tscal[:, 0:1], ALU.mult).then_inc(coef_step, 1)
            pool.tensor_tensor(coef[:, 1:2], coef[:, 0:1], tscal[:, 0:1], ALU.mult).then_inc(coef_step, 1)
            pool.wait_ge(coef_step, 4)
            ln1_coefficients(0)
            pool.tensor_copy(gw_hi[:, :], gw_raw).then_inc(gw_split, 1)
            pool.wait_ge(gw_split, 1)
            pool.tensor_tensor(gw_lo[:, :], gw_raw, gw_hi[:, :].bitcast(F32), ALU.subtract).then_inc(gw_split, 1)
            for n in range(EARLY):
                weights_lo(n)
                if n == EARLY - 2:
                    rstd2(0)
            ln1_coefficients(1)
            for s in range(NSLOT):
                g, m = s // SLOTS, s % SLOTS
                if g == 0 and EARLY + m < len(PIECES):
                    weights_lo(EARLY + m)
                if m == 1 and g >= 1 and g + 1 < NB:
                    ln1_coefficients(g + 1)
                if m == 6 and g + 1 < NB:
                    rstd2(g + 1)
                hidden_lo(s)


_SHAPE = (NB, NTOK, D)


def kernel(x, ctx_512, g_xattn, g_ffn, L0_xattn_Wq, L0_xattn_Wk, L0_xattn_gamma_raw, L0_ffn_gate_w, L0_ffn_w_gate,
           L0_ffn_w_up, L0_ffn_w_down, L0_ffn_sw_gate, L0_ffn_sw_up, L0_ffn_sw_down, L0_ffn_shared_gate_w):
    import numpy as np
    import concourse.bacc as bacc
    from concourse.bass_utils import run_bass_kernel_spmd

    f = np.float32
    a = np.asarray
    gate = np.concatenate([a(L0_ffn_w_gate).transpose(1, 0, 2).reshape(D, E * EI), a(L0_ffn_sw_gate)], axis=1)
    up = np.concatenate([a(L0_ffn_w_up).transpose(1, 0, 2).reshape(D, E * EI), a(L0_ffn_sw_up)], axis=1)
    down = np.concatenate([a(L0_ffn_w_down).reshape(E * EI, D), a(L0_ffn_sw_down)], axis=0)
    whole = CHUNKS * P
    gu = np.stack([gate[:, :whole], up[:, :whole]]).reshape(2, KD, P, CHUNKS, P).transpose(2, 3, 0, 1, 4)
    wd = down[:whole].reshape(CHUNKS, P, D).transpose(1, 0, 2)
    wpack = np.zeros((P, WCOLS), f)
    for n, (kind, c) in enumerate(PIECES):
        at = n * PIECE
        if kind == "gu":
            wpack[:, at:at + PIECE] = gu[:, c:c + 2].reshape(P, PIECE)
        elif kind == "wd":
            wpack[:, at:at + PIECE] = wd[:, c:c + 4].reshape(P, PIECE)
        else:
            both = np.concatenate([gate[:, whole:], up[:, whole:]], axis=1)
            wpack[:, at:at + 256] = both.reshape(KD, P, P).transpose(1, 0, 2).reshape(P, KD * P)
            wpack[P - TAIL:, at + 256:at + 512] = down[whole:]
    const = np.zeros((P, CONST), f)
    const[:, 0:P] = np.eye(P, dtype=f)
    const[:, C_IOTA:C_IOTA + 8] = np.arange(8, dtype=f)
    const[:, C_HALF] = -0.5
    for n, v in enumerate((g_xattn, g_ffn, L0_xattn_gamma_raw)):
        const[:, C_SCAL + n] = a(v).reshape(-1)[0]
    gw = const[:, C_GW:].reshape(P, KD, CW)
    gw[:, :, 0:E] = a(L0_ffn_gate_w).T.reshape(KD, P, E).transpose(1, 0, 2)
    gw[:, :, E] = a(L0_ffn_shared_gate_w).reshape(KD, P).T
    const[:, C_GW:] = gw.reshape(P, KD * CW)
    sel = np.zeros((2, CW, MOE_CH * P), f)
    sel[:, np.arange(E * EI) // EI, np.arange(E * EI)] = 1
    arrays = {
        "x": np.ascontiguousarray(x),
        "qk_in": np.concatenate([a(L0_xattn_Wq).T, a(L0_xattn_Wk).T,
                                 a(ctx_512).transpose(2, 0, 1).reshape(DC, NB * NTOK)], axis=1),
        "sel": sel.reshape(2 * CW, MOE_CH * P),
        "const": const,
        "wpack": wpack,
    }
    nc = bacc.Bacc("TRN2", target_bir_lowering=False, num_devices=1)
    aps = [nc.dram_tensor(n, v.shape, mybir.dt.from_np(v.dtype), kind="ExternalInput").ap() for n, v in arrays.items()]
    out = nc.dram_tensor("out", _SHAPE, F32, kind="ExternalOutput").ap()
    build(nc, *aps, out)
    r = run_bass_kernel_spmd(nc, [arrays], core_ids=[0])
    return r.results[0]["out"]
```

```python
from contextlib import ExitStack

import concourse.bass as bass
from concourse import mybir

ALU = mybir.AluOpType
ACT = mybir.ActivationFunctionType
F32 = mybir.dt.float32
F32R = mybir.dt.float32r
U32 = mybir.dt.uint32

P = 128
NB, NTOK, D, DC = 4, 256, 256, 64
KD = D // P
E, EI, SI = 8, 176, 704
MOE_CH = E * EI // P
CHUNKS = (E * EI + SI) // P
SH_CH = CHUNKS - MOE_CH
TAIL = E * EI + SI - CHUNKS * P
PAIRS = CHUNKS // 2
SLOTS = PAIRS + 1
TOPK = int(NTOK * 0.3)
ROUNDS = (TOPK + 7) // 8
EPS = 1e-5
CW = 10
TOPK_DONE = [1, 2, 4, 6, 8, ROUNDS]
C_SLOT = SH_CH // 2
C_SLOTS = PAIRS - C_SLOT
BIG = 3.0e38
assert 2 * PAIRS == CHUNKS and TAIL == 64 and NTOK == 2 * P

PIECE = 1024
PIECES = []
for _q in range(CHUNKS // 4):
    PIECES += [("gu", 4 * _q), ("gu", 4 * _q + 2), ("wd", 4 * _q)]
PIECES += [("tail", CHUNKS)]
C_IOTA, C_HALF, C_SCAL, C_GW = P, P + 8, P + 9, P + 12
CONST = C_GW + KD * CW
WCOLS = PIECE * (len(PIECES) - 1) + 512
RING = 5
EARLY = 7
WARM_LOAD, WARM_COPY, WARM_TOPK, WARM_Y = 7, 3, 7, 12


def gu_at(chunk):
    n = PIECES.index(("tail", CHUNKS) if chunk == CHUNKS else ("gu", chunk - chunk % 2))
    return n, n * PIECE + (0 if chunk == CHUNKS else 512 * (chunk % 2))


def wd_at(chunk):
    n = PIECES.index(("tail", CHUNKS) if chunk == CHUNKS else ("wd", chunk - chunk % 4))
    return n, n * PIECE + (256 if chunk == CHUNKS else 256 * (chunk % 4))


def is_expert(chunk):
    return SH_CH <= chunk < CHUNKS


def expert_rows(chunk):
    first = (chunk - SH_CH) * P
    return [(e, max(e * EI - first, 0), min((e + 1) * EI - first, P))
            for e in range(first // EI, (first + P - 1) // EI + 1)]


def build(nc, x, qk_in, const, wpack, out):
    x_v = x.rearrange("b (r p) d -> p (b r) d", p=P)
    out_v = out.rearrange("b (r p) d -> p (b r) d", p=P)
    NSLOT = NB * SLOTS

    with ExitStack() as ctx:
        def sb(name, shape, dt=F32):
            return ctx.enter_context(nc.sbuf_tensor(name, shape, dt))

        def sem(name):
            return ctx.enter_context(nc.semaphore(name))

        def bank(name):
            return ctx.enter_context(nc.psum_tensor(name, [P, 512], F32))

        gate_ps = [bank("gate0"), bank("gate1")]
        up_ps = [bank("up0"), bank("up1")]
        sim_ps = bank("sim_ps")
        down_ps = [bank("down0"), bank("down1")]
        misc_ps = bank("misc")

        xs = sb("xs", [P, 2 * NB, D])
        qk_sb = sb("qk_sb", [DC, 2 * DC + NB * NTOK])
        w_qk = qk_sb[:, 0:2 * DC]
        ctxT = qk_sb[:, 2 * DC:]
        qT = sb("qT", [DC, NB * NTOK])
        kT = sb("kT", [DC, NB * NTOK])
        const_sb = sb("const_sb", [P, CONST])
        ident = const_sb[:, 0:P]
        iota8 = const_sb[:, C_IOTA:C_IOTA + 8]
        minus_half = const_sb[:, C_HALF:C_HALF + 1]
        scal_sb = const_sb[:, C_SCAL:C_SCAL + 3]
        gw_raw = const_sb[:, C_GW:C_GW + KD * CW]
        idle = sb("idle", [P, 512], mybir.dt.bfloat16)
        tscal = sb("tscal", [P, 3])
        coef = sb("coef", [P, 4])
        c_res, c_adj, c_ffn = coef[:, 1:2], coef[:, 2:3], tscal[:, 1:2]
        gw = sb("gw", [P, KD, 2 * CW], F32R)
        shared_w = sb("shared_w", [P, NB, 2])
        raw = sb("raw", [P, RING, PIECE])
        w_hi = sb("w_hi", [P, WCOLS], F32R)
        w_lo = sb("w_lo", [P, WCOLS], F32R)
        sim = sb("sim", [P, NB, 2, NTOK])
        work = sb("work", [P, 2, NTOK])
        top8 = sb("top8", [P, 2, 8])
        th1 = sb("th1", [P, 2, NTOK])
        adj = sb("adj", [P, 2, NTOK])
        st1 = sb("st1", [P, 2, 6])
        mv1 = sb("mv1", [P, NB, 2, 2])
        ln1 = sb("ln1", [P, NB, 4, 2])
        st2 = sb("st2", [P, 2, 6])
        mv2 = sb("mv2", [P, 2, 2])
        rs2 = sb("rs2", [P, 2, 2])
        y = sb("y", [P, 2, D])
        yT_hi = sb("yT_hi", [P, NB, 2 * NTOK], F32R)
        yT_lo = sb("yT_lo", [P, NB, 2 * NTOK], F32R)
        lg = sb("lg", [P, 2, CW])
        lmax = sb("lmax", [P, 2, 8])
        lidx = sb("lidx", [P, 2, 8], U32)
        lidf = sb("lidf", [P, 2, 2])
        dz = sb("dz", [P, 2, 2])
        tdz = sb("tdz", [P, 2, 2])
        wts = sb("wts", [P, 2, 3])
        pick = sb("pick", [P, 2, 2, E])
        comb = sb("comb", [P, 2, E])
        cT = sb("cT", [E, NTOK])
        c_all = sb("c_all", [P, MOE_CH, NTOK])
        act_in = sb("act_in", [P, 1])
        act_out = sb("act_out", [P, 1])
        silu_sb = sb("silu_sb", [P, 2, 512])
        h32 = sb("h32", [P, 2, 512])
        h_hi = sb("h_hi", [P, 3, 512], F32R)
        h_lo = sb("h_lo", [P, 3, 512], F32R)

        qk0_in, ctx_in, const_in = (sem(n) for n in ("qk0_in", "ctx_in", "const_in"))
        c_in = [sem(f"c_in{m}") for m in range(C_SLOT, PAIRS)]
        x_in = [sem(f"x_in{b}") for b in range(NB)]
        raw_in = [sem(f"raw_in{s}") for s in range(RING)]
        out_sent = sem("out_sent")
        qk_ready, sim_ready, adjT_ready, yT_ready, logit_ready, cT_ready = (sem(n) for n in (
            "qk_ready", "sim_ready", "adjT_ready", "yT_ready", "logit_ready", "cT_ready"))
        gu_ready, down_done = sem("gu_ready"), sem("down_done")
        tscal_done, q_copied, sim_copied, tanh_done, th1_done, base_done = (sem(n) for n in (
            "tscal_done", "q_copied", "sim_copied", "tanh_done", "th1_done", "base_done"))
        yhi_done, tdz_done, cT_copied, silu_done, hhi_done, whi_done = (sem(n) for n in (
            "yhi_done", "tdz_done", "cT_copied", "silu_done", "hhi_done", "whi_done"))
        zeroed, xstat_step, mv1_done, topk_step, adj_done, x2a_done, x2_done = (sem(n) for n in (
            "zeroed", "xstat_step", "mv1_done", "topk_step", "adj_done", "x2a_done", "x2_done"))
        stat2_step, mv2_done, y_done, ylo_done, route_step, dz_done, comb_done = (sem(n) for n in (
            "stat2_step", "mv2_done", "y_done", "ylo_done", "route_step", "dz_done", "comb_done"))
        t2_done, hid_done, moe_added, out_done, k_copied, shared_done = (sem(n) for n in (
            "t2_done", "hid_done", "moe_added", "out_done", "k_copied", "shared_done"))
        lg_copied, tail_lo_done = sem("lg_copied"), sem("tail_lo_done")
        gw_split, coef_step, ln1_step, ln1_done = (sem(n) for n in (
            "gw_split", "coef_step", "ln1_step", "ln1_done"))
        rs2_step, rs2_done, wlo_done, hlo_done = (sem(n) for n in (
            "rs2_step", "rs2_done", "wlo_done", "hlo_done"))

        def later_sim_bank(b):
            return {1: sim_ps, 2: down_ps[0], 3: up_ps[1]}[b]

        def sim_bank(b, r):
            if b == 0:
                return (misc_ps, down_ps[1])[r][:, 0:NTOK]
            return later_sim_bank(b)[:, r * NTOK:(r + 1) * NTOK]

        def batches_of_sim(b):
            return b + 2

        def yT_bank(b, k):
            return down_ps[0][:, 0:NTOK] if b == 0 and k == 1 else misc_ps[:, k * NTOK:(k + 1) * NTOK]

        def halves_of_y(b, k):
            return 1 + k if b == 0 else b + 2

        def qk_bank(b):
            return (up_ps[1], gate_ps[0], gate_ps[1], up_ps[0])[b]

        def hidden_made(eng, s):
            if C_SLOT <= s % SLOTS < PAIRS:
                eng.wait_ge(hid_done, s // SLOTS * C_SLOTS + s % SLOTS - C_SLOT + 1)
            else:
                eng.wait_ge(t2_done, s + 1)

        def low_made(eng, s):
            if s % SLOTS == PAIRS:
                eng.wait_ge(tail_lo_done, s // SLOTS + 1)
            else:
                eng.wait_ge(hlo_done, s // SLOTS * PAIRS + s % SLOTS + 1)

        block = ctx.enter_context(nc.Block())

        @block.sync
        def _(sp):
            def spread_c(b):
                sp.wait_ge(cT_copied, b + 1)
                if b >= 1:
                    sp.wait_ge(hid_done, C_SLOTS * b)
                for chunk in range(SH_CH, CHUNKS):
                    for e, lo, hi in expert_rows(chunk):
                        sp.dma_start(c_all[lo:hi, chunk - SH_CH, :],
                                     cT[e:e + 1, None, :].to_broadcast([1, hi - lo, NTOK])).then_inc(
                                         c_in[chunk // 2 - C_SLOT], 16)

            first = 2 * DC + NTOK
            sp.dma_start(qk_sb[:, 0:first], qk_in[:, 0:first]).then_inc(qk0_in, 16)
            sp.dma_start(xs[:, 0:2, :], x_v[:, 0:2, :]).then_inc(x_in[0], 16)
            for n in range(len(PIECES)):
                if n == len(PIECES) - 1:
                    spread_c(0)
                if n >= RING:
                    sp.wait_ge(wlo_done, n - RING + 1)
                w = min(PIECE, WCOLS - n * PIECE)
                sp.dma_start(raw[:, n % RING, 0:w], wpack[:, n * PIECE:n * PIECE + w]).then_inc(raw_in[n % RING], 16)
                if n == 0:
                    sp.dma_start(qk_sb[:, first:], qk_in[:, first:]).then_inc(ctx_in, 16)
                if 1 <= n < NB:
                    b = n
                    sp.dma_start(xs[:, 2 * b:2 * b + 2, :], x_v[:, 2 * b:2 * b + 2, :]).then_inc(x_in[b], 16)
            for b in range(NB):
                if b + 1 < NB:
                    spread_c(b + 1)
                for i in (2 * b, 2 * b + 1):
                    sp.wait_ge(out_done, i + 1)
                    sp.dma_start(out_v[:, i, :], xs[:, i, :]).then_inc(out_sent, 16)
            sp.wait_ge(out_sent, 16 * 2 * NB)

        @block.tensor
        def _(pe):
            def query_key(b, ps):
                pe.matmul(ps[:, 0:NTOK], w_qk, ctxT[:, b * NTOK:(b + 1) * NTOK],
                          start=True, stop=True).then_inc(qk_ready, 1)

            def similarity(b):
                pe.wait_ge(q_copied, b + 1)
                pe.wait_ge(k_copied, b + 1)
                for r in range(2):
                    i = 2 * b + r
                    pe.matmul(sim_bank(b, r), qT[:, i * P:(i + 1) * P], kT[:, b * NTOK:(b + 1) * NTOK],
                              start=True, stop=True).then_inc(sim_ready, 1)

            def transpose_adj(b):
                for c in range(2):
                    pe.wait_ge(adj_done, 2 * b + c + 1)
                    for r in range(2):
                        last = pe.transpose(misc_ps[:, r * NTOK + c * P:r * NTOK + (c + 1) * P],
                                            adj[:, c, r * P:(r + 1) * P], ident)
                last.then_inc(adjT_ready, 1)

            def transpose_y(b):
                for r in range(2):
                    pe.wait_ge(y_done, 2 * b + r + 1)
                    for k in range(KD):
                        half = pe.transpose(yT_bank(b, k)[:, r * P:(r + 1) * P], y[:, r, k * P:(k + 1) * P], ident)
                        if r == 1:
                            half.then_inc(yT_ready, 1)

            def logits(b):
                pe.wait_ge(yhi_done, halves_of_y(b, 1))
                pe.wait_ge(ylo_done, halves_of_y(b, 1))
                pe.wait_ge(gw_split, 2)
                for r in range(2):
                    for k in range(KD):
                        at = slice(k * NTOK + r * P, k * NTOK + (r + 1) * P)
                        base = r * 2 * CW
                        pe.matmul(misc_ps[:, base:base + 2 * CW], yT_hi[:, b, at], gw[:, k, :],
                                  start=(k == 0), stop=False, skip_group_check=True)
                        last = pe.matmul(misc_ps[:, base:base + CW], yT_lo[:, b, at], gw[:, k, 0:CW],
                                         start=False, stop=(k == KD - 1), skip_group_check=True)
                last.then_inc(logit_ready, 1)

            def transpose_comb(b):
                pe.wait_ge(comb_done, b + 1)
                for r in range(2):
                    last = pe.transpose(misc_ps[0:E, r * P:(r + 1) * P], comb[:, r, :], ident)
                last.then_inc(cT_ready, 1)

            def gate_up(s, between=None):
                g, m = s // SLOTS, s % SLOTS
                if s >= 2:
                    pe.wait_ge(silu_done, s - 1)
                    pe.wait_ge(t2_done, s - 1)
                chunks = (2 * m, 2 * m + 1) if m < PAIRS else (CHUNKS,)
                for q, c in enumerate(chunks):
                    n, col = gu_at(c)
                    if g == 0:
                        pe.wait_ge(whi_done, n + 1)
                        pe.wait_ge(wlo_done, n + 1)
                    banks = (gate_ps, up_ps) if m < PAIRS else (gate_ps,)
                    for y_part, made, parts in ((yT_hi, yhi_done, (w_hi, w_lo)), (yT_lo, ylo_done, (w_hi,))):
                        for half, dst in enumerate(banks):
                            for k in range(KD):
                                if m == 0 and q == 0 and half == 0:
                                    pe.wait_ge(made, halves_of_y(g, k))
                                wk = slice(col + (half * KD + k) * P, col + (half * KD + k + 1) * P)
                                for w in parts:
                                    last = pe.matmul(dst[s % 2][:, q * NTOK:(q + 1) * NTOK], w[:, wk],
                                                     y_part[:, g, k * NTOK:(k + 1) * NTOK],
                                                     start=(y_part is yT_hi and k == 0 and w is w_hi),
                                                     stop=(y_part is yT_lo and k == KD - 1))
                    if q == 0 and between is not None:
                        between()
                last.then_inc(gu_ready, 1)

            def down(s):
                g, m = s // SLOTS, s % SLOTS
                pe.wait_ge(hhi_done, s + 1)
                if m == 0 and g >= 1:
                    pe.wait_ge(out_done, 2 * g)
                if m == C_SLOT and g >= 1:
                    pe.wait_ge(moe_added, g)
                chunks = (2 * m, 2 * m + 1)
                if g == 0:
                    piece = wd_at(chunks[-1] if m < PAIRS else CHUNKS)[0]
                    pe.wait_ge(whi_done, piece + 1)
                    pe.wait_ge(wlo_done, piece + 1)
                if m == PAIRS:
                    col = wd_at(CHUNKS)[1]
                    for n, (rows, w) in enumerate(((slice(P - TAIL, P), w_lo), (slice(0, P), w_hi))):
                        if n == 1:
                            low_made(pe, s)
                        for r in range(2):
                            last = pe.matmul(down_ps[1][:, r * D:(r + 1) * D], h_hi[rows, s % 3, r * P:(r + 1) * P],
                                             w[rows, col:col + D], start=False, stop=(n == 1), skip_group_check=True)
                    last.then_inc(down_done, 1)
                    return
                for h, parts in ((h_hi, (w_hi, w_lo)), (h_lo, (w_hi,))):
                    if h is h_lo:
                        low_made(pe, s)
                    for q, c in enumerate(chunks):
                        wc = slice(wd_at(c)[1], wd_at(c)[1] + D)
                        for r in range(2):
                            for w in parts:
                                last = pe.matmul(down_ps[0 if is_expert(c) else 1][:, r * D:(r + 1) * D],
                                                 h[:, s % 3, q * NTOK + r * P:q * NTOK + (r + 1) * P], w[:, wc],
                                                 start=(c in (0, SH_CH) and r == 0 and h is h_hi and w is w_hi),
                                                 stop=(c == CHUNKS - 1 and h is h_lo),
                                                 skip_group_check=True)
                last.then_inc(down_done, 1)

            def keep_warm(n):
                for _ in range(n):
                    pe.matmul(gate_ps[0][:, :], idle[:, 0:P], idle[:, :], start=True, stop=True)

            pe.wait_ge(zeroed, 1)
            keep_warm(WARM_LOAD)
            pe.wait_ge(qk0_in, 16)
            query_key(0, qk_bank(0))
            keep_warm(WARM_COPY)
            similarity(0)
            pe.wait_ge(ctx_in, 16)
            for b in range(1, NB):
                query_key(b, qk_bank(b))
            for b in range(1, NB):
                similarity(b)
            pe.wait_ge(topk_step, 4 * (ROUNDS - 4))
            keep_warm(WARM_TOPK)
            pe.wait_ge(const_in, 16)
            transpose_adj(0)
            keep_warm(WARM_Y)
            pe.wait_ge(x2_done, 1)
            transpose_y(0)
            pe.wait_ge(sim_copied, batches_of_sim(NB - 1))
            for s in range(NSLOT):
                g, m = s // SLOTS, s % SLOTS
                gate_up(s, between={0: lambda: logits(g), 1: lambda: transpose_comb(g)}.get(m))
                if m == 8 and g + 1 < NB:
                    transpose_y(g + 1)
                if s >= 2:
                    down(s - 2)
                if m == 6 and g + 1 < NB:
                    pe.wait_ge(cT_copied, g + 1)
                    transpose_adj(g + 1)
            down(NSLOT - 2)
            down(NSLOT - 1)

        @block.scalar
        def _(act):
            def weights_hi(n):
                w = min(PIECE, WCOLS - n * PIECE)
                act.wait_ge(raw_in[n % RING], 16 * (n // RING + 1))
                act.activation(w_hi[:, n * PIECE:n * PIECE + w], raw[:, n % RING, 0:w], ACT.Copy).then_inc(whi_done, 1)

            def copy_q(b):
                act.wait_ge(qk_ready, b + 1)
                act.activation(qT[:, b * NTOK:(b + 1) * NTOK], qk_bank(b)[0:DC, 0:NTOK], ACT.Copy).then_inc(q_copied, 1)

            def copy_k(b):
                act.activation(kT[:, b * NTOK:(b + 1) * NTOK], qk_bank(b)[DC:2 * DC, 0:NTOK], ACT.Copy).then_inc(k_copied, 1)

            def copy_sim(b):
                if b == 0:
                    for r in range(2):
                        act.wait_ge(topk_step, 3 + r)
                        act.activation(sim[:, 0, r, :], sim_bank(0, r), ACT.Copy).then_inc(sim_copied, 1)
                else:
                    act.wait_ge(sim_ready, 2 * b + 2)
                    act.activation(sim[:, b, :, :], later_sim_bank(b)[:, :], ACT.Copy).then_inc(sim_copied, 1)

            def tanh_sim(b):
                act.wait_ge(sim_copied, batches_of_sim(b))
                if b >= 1:
                    act.wait_ge(adj_done, 2 * b)
                act.activation(th1[:, :, :], sim[:, b, :, :], ACT.Tanh, scale=1.0 / 32).then_inc(tanh_done, 1)
                act.wait_ge(tanh_done, b + 1)
                act.activation(th1[:, :, :], th1[:, :, :], ACT.Copy, bias=1.0).then_inc(th1_done, 1)

            def residual_base(b):
                act.wait_ge(ln1_done, b + 1)
                for r in range(2):
                    act.activation(xs[:, 2 * b + r, :], xs[:, 2 * b + r, :], ACT.Identity,
                                   bias=ln1[:, b, 3, r:r + 1], scale=ln1[:, b, 2, r:r + 1]).then_inc(base_done, 1)

            def split_y(b):
                if b == 0:
                    for k in range(KD):
                        act.wait_ge(yT_ready, k + 1)
                        act.activation(yT_hi[:, 0, k * NTOK:(k + 1) * NTOK], yT_bank(0, k), ACT.Copy).then_inc(yhi_done, 1)
                else:
                    act.wait_ge(yT_ready, KD * (b + 1))
                    act.activation(yT_hi[:, b, :], misc_ps[:, :], ACT.Copy).then_inc(yhi_done, 1)

            def copy_cT(b):
                act.wait_ge(cT_ready, b + 1)
                if b >= 1:
                    act.wait_ge(hid_done, C_SLOTS * b)
                act.activation(cT[:, :], misc_ps[0:E, 0:NTOK], ACT.Copy).then_inc(cT_copied, 1)

            def silu(s):
                act.wait_ge(gu_ready, s + 1)
                if s >= 2:
                    act.wait_ge(t2_done, s - 1)
                if s % SLOTS < PAIRS:
                    act.activation(silu_sb[:, s % 2, :], gate_ps[s % 2][:, :], ACT.Silu).then_inc(silu_done, 1)
                else:
                    act.activation(silu_sb[P - TAIL:P, s % 2, 0:NTOK], gate_ps[s % 2][0:TAIL, 0:NTOK],
                                   ACT.Silu).then_inc(silu_done, 1)

            def hidden_hi(s):
                hidden_made(act, s)
                if s >= 3:
                    act.wait_ge(down_done, s - 2)
                rows, cols = (slice(0, P), 512) if s % SLOTS < PAIRS else (slice(P - TAIL, P), NTOK)
                act.activation(h_hi[rows, s % 3, 0:cols], h32[rows, s % 2, 0:cols], ACT.Copy).then_inc(hhi_done, 1)

            act.wait_ge(zeroed, 2)
            act.activation(act_out[:, :], act_in[:, :], ACT.Silu)
            act.wait_ge(const_in, 16)
            act.activation(tscal[:, 0:2], scal_sb[:, 0:2], ACT.Tanh).then_inc(tscal_done, 1)
            act.activation(tscal[:, 2:3], scal_sb[:, 2:3], ACT.Tanh, scale=0.5).then_inc(tscal_done, 1)
            copy_q(0)
            weights_hi(0)
            copy_sim(0)
            tanh_sim(0)
            for n in range(1, EARLY):
                weights_hi(n)
                if n == 1:
                    for b in range(1, NB):
                        copy_q(b)
                        copy_k(b)
                if n == 2:
                    residual_base(0)
                if 2 <= n <= NB:
                    copy_sim(n - 1)
            split_y(0)
            tanh_sim(1)
            for s in range(NSLOT):
                g, m = s // SLOTS, s % SLOTS
                if m == 0:
                    act.wait_ge(dz_done, g + 1)
                    act.activation(tdz[:, :, :], dz[:, :, :], ACT.Tanh, scale=0.5).then_inc(tdz_done, 1)
                if m == 1:
                    copy_cT(g)
                silu(s)
                if g == 0 and EARLY + m < len(PIECES):
                    weights_hi(EARLY + m)
                if m == 3 and g + 1 < NB:
                    residual_base(g + 1)
                if m == 8 and g + 1 < NB:
                    split_y(g + 1)
                if m == 8 and g + 1 < NB:
                    hidden_hi(s - 1)
                if m != 7 or g + 1 == NB:
                    hidden_hi(s)
                if m == 8 and g + 2 < NB:
                    tanh_sim(g + 2)

        @block.vector
        def _(dve):
            def stats(tile, st, mv, step, done, count):
                for r in range(2):
                    dve.bn_stats(st[:, r, :], tile[:, r, :]).then_inc(step, 1)
                for r in range(2):
                    dve.wait_ge(step, 2 * count + r + 1)
                    dve.bn_aggr(mv[:, r, :], st[:, r, :]).then_inc(done, 1)

            def x_stats(b):
                dve.wait_ge(x_in[b], 16)
                if b >= 1:
                    dve.wait_ge(mv1_done, 2 * b)
                stats(xs[:, 2 * b:2 * b + 2, :], st1, mv1[:, b, :, :], xstat_step, mv1_done, b)

            def topk_rounds(b, first, end):
                def follow(n):
                    if n >= 2:
                        dve.wait_ge(topk_step, n - 1)

                def source(k, r):
                    if k > 0:
                        return work[:, r, :]
                    return sim_bank(0, r) if b == 0 else sim[:, b, r, :]

                for k in range(first, end):
                    n = b * (4 * ROUNDS - 2) + 4 * k
                    for r in range(2):
                        if k == 0:
                            dve.wait_ge(*((sim_ready, r + 1) if b == 0 else (sim_copied, batches_of_sim(b))))
                        follow(n + r)
                        dve.max(top8[:, r, :], source(k, r)).then_inc(topk_step, 1)
                    if k < ROUNDS - 1:
                        for r in range(2):
                            follow(n + 2 + r)
                            dve.match_replace(work[:, r, :], top8[:, r, :], source(k, r),
                                              -BIG).then_inc(topk_step, 1)

            def adjacency(b):
                kth = TOPK - 8 * (ROUNDS - 1) - 1
                dve.wait_ge(th1_done, b + 1)
                if b >= 1:
                    dve.wait_ge(adjT_ready, b)
                for r in range(2):
                    dve.wait_ge(topk_step, (b + 1) * (4 * ROUNDS - 2) - 1 + r)
                    dve.scalar_tensor_tensor(adj[:, r, :], sim[:, b, r, :], top8[:, r, kth:kth + 1], th1[:, r, :],
                                             ALU.is_ge, ALU.mult).then_inc(adj_done, 1)
                dve.wait_ge(adj_done, 2 * (b + 1))
                dve.wait_ge(base_done, 2 * (b + 1))
                xb = xs[:, 2 * b:2 * b + 2, :]
                dve.scalar_tensor_tensor(xb, adj[:, :, :], c_adj, xb, ALU.mult, ALU.add).then_inc(x2a_done, 1)

            def finish_x2(b):
                xb = xs[:, 2 * b:2 * b + 2, :]
                dve.wait_ge(x2a_done, b + 1)
                dve.wait_ge(adjT_ready, b + 1)
                dve.scalar_tensor_tensor(xb, misc_ps[:, :].rearrange("p (r n) -> p r n", r=2), c_adj, xb,
                                         ALU.mult, ALU.add).then_inc(x2_done, 1)
                dve.wait_ge(x2_done, b + 1)
                stats(xb, st2, mv2, stat2_step, mv2_done, b)

            def normalise(b):
                dve.wait_ge(rs2_done, b + 1)
                if b >= 1:
                    dve.wait_ge(yT_ready, KD * b)
                for r in range(2):
                    dve.tensor_scalar(y[:, r, :], xs[:, 2 * b + r, :], mv2[:, r, 0:1], rs2[:, 1, r:r + 1],
                                      ALU.subtract, ALU.mult).then_inc(y_done, 1)

            def y_lo(b):
                if b == 0:
                    for k in range(KD):
                        at = slice(k * NTOK, (k + 1) * NTOK)
                        dve.wait_ge(yhi_done, halves_of_y(0, k))
                        dve.tensor_tensor(yT_lo[:, 0, at], yT_bank(0, k), yT_hi[:, 0, at].bitcast(F32),
                                          ALU.subtract).then_inc(ylo_done, 1)
                else:
                    dve.wait_ge(yhi_done, halves_of_y(b, 1))
                    dve.tensor_tensor(yT_lo[:, b, :], misc_ps[:, :], yT_hi[:, b, :].bitcast(F32),
                                      ALU.subtract).then_inc(ylo_done, 1)

            ROUTE = 11

            def route_first(b):
                n = b * ROUTE
                dve.wait_ge(logit_ready, b + 1)
                both = misc_ps[:, 0:4 * CW].rearrange("p (r h e) -> p r h e", r=2, h=2)
                dve.tensor_copy(lg[:, :, :], both[:, :, 0, :]).then_inc(lg_copied, 1)
                dve.wait_ge(lg_copied, b + 1)
                dve.tensor_tensor(lg[:, :, :], both[:, :, 1, :], lg[:, :, :], ALU.add).then_inc(route_step, 1)
                dve.wait_ge(route_step, n + 1)
                for r in range(2):
                    dve.max(lmax[:, r, :], lg[:, r, 0:E]).then_inc(route_step, 1)
                dve.wait_ge(route_step, n + 3)
                dve.tensor_tensor(dz[:, :, 1:2], lmax[:, :, 0:1], lmax[:, :, 1:2], ALU.subtract).then_inc(route_step, 1)
                dve.wait_ge(route_step, n + 4)
                dve.tensor_copy(dz[:, :, 0:1], lg[:, :, E:E + 1]).then_inc(dz_done, 1)
                for r in range(2):
                    dve.max_index(lidx[:, r, :], lmax[:, r, :], lg[:, r, 0:E]).then_inc(route_step, 1)
                dve.wait_ge(route_step, n + 6)
                dve.tensor_copy(lidf[:, :, :], lidx[:, :, 0:2]).then_inc(route_step, 1)
                dve.wait_ge(route_step, n + 7)
                dve.tensor_tensor(pick[:, :, :, :], iota8[:, None, None, :].to_broadcast([P, 2, 2, E]),
                                  lidf[:, :, :, None].to_broadcast([P, 2, 2, E]), ALU.is_equal).then_inc(route_step, 1)

            def route_second(b):
                n = b * ROUTE + 8
                dve.wait_ge(tdz_done, b + 1)
                dve.tensor_scalar(wts[:, :, 0:2], tdz[:, :, :], 0.5, 0.5, ALU.mult, ALU.add).then_inc(route_step, 1)
                dve.tensor_scalar(wts[:, :, 2:3], tdz[:, :, 1:2], -0.5, 0.5, ALU.mult, ALU.add).then_inc(route_step, 1)
                dve.wait_ge(route_step, n + 2)
                dve.tensor_tensor(pick[:, :, :, :], pick[:, :, :, :], wts[:, :, 1:3, None].to_broadcast([P, 2, 2, E]),
                                  ALU.mult).then_inc(route_step, 1)
                dve.wait_ge(route_step, n + 3)
                if b >= 1:
                    dve.wait_ge(cT_ready, b)
                dve.tensor_tensor(comb[:, :, :], pick[:, :, 0, :], pick[:, :, 1, :], ALU.add).then_inc(comb_done, 1)
                dve.tensor_scalar(shared_w[:, b, :], wts[:, :, 0], c_ffn, None, ALU.mult).then_inc(shared_done, 1)

            def hidden_up(s):
                g, m = s // SLOTS, s % SLOTS
                rows, cols, up = (slice(0, P), 512, up_ps) if m < PAIRS else (slice(P - TAIL, P), NTOK, gate_ps)
                dve.wait_ge(silu_done, s + 1)
                if s >= 2:
                    low_made(dve, s - 2)
                h = h32[rows, s % 2, 0:cols]
                dve.tensor_tensor(h, silu_sb[rows, s % 2, 0:cols], up[s % 2][rows, 0:cols], ALU.mult).then_inc(t2_done, 1)

            def hidden_c(s):
                g, m = s // SLOTS, s % SLOTS
                if not C_SLOT <= m < PAIRS:
                    return
                first = max(2 * m, SH_CH)
                chunks = 2 * m + 2 - first
                dve.wait_ge(t2_done, s + 1)
                dve.wait_ge(c_in[m - C_SLOT], 16 * (g + 1) * sum(len(expert_rows(first + n)) for n in range(chunks)))
                h = h32[:, s % 2, (first - 2 * m) * NTOK:2 * NTOK].rearrange("p (q n) -> p q n", n=NTOK)
                dve.tensor_tensor(h, h, c_all[:, first - SH_CH:first - SH_CH + chunks, :], ALU.mult).then_inc(hid_done, 1)

            def tail_lo(g):
                s = g * SLOTS + PAIRS
                dve.wait_ge(hhi_done, s + 1)
                dve.wait_ge(down_done, s - 2)
                dve.tensor_tensor(h_hi[0:TAIL, s % 3, 0:NTOK], h32[P - TAIL:P, s % 2, 0:NTOK],
                                  h_hi[P - TAIL:P, s % 3, 0:NTOK].bitcast(F32), ALU.subtract).then_inc(tail_lo_done, 1)

            def add_moe(b):
                xb = xs[:, 2 * b:2 * b + 2, :]
                dve.wait_ge(down_done, SLOTS * b + PAIRS)
                dve.scalar_tensor_tensor(xb, down_ps[0][:, :].rearrange("p (r n) -> p r n", r=2), c_ffn, xb,
                                         ALU.mult, ALU.add).then_inc(moe_added, 1)

            def add_shared(b):
                dve.wait_ge(moe_added, b + 1)
                dve.wait_ge(shared_done, b + 1)
                dve.wait_ge(down_done, SLOTS * (b + 1))
                for r in range(2):
                    xr = xs[:, 2 * b + r, :]
                    dve.scalar_tensor_tensor(xr, down_ps[1][:, r * D:(r + 1) * D], shared_w[:, b, r:r + 1], xr,
                                             ALU.mult, ALU.add).then_inc(out_done, 1)

            dve.memset(idle[:, :], 0.0).then_inc(zeroed, 1)
            dve.memset(act_in[:, :], 0.0).then_inc(zeroed, 1)
            dve.wait_ge(qk_ready, 1)
            dve.tensor_copy(kT[:, 0:NTOK], qk_bank(0)[DC:2 * DC, 0:NTOK]).then_inc(k_copied, 1)
            x_stats(0)
            topk_rounds(0, 0, ROUNDS)
            adjacency(0)
            finish_x2(0)
            x_stats(1)
            normalise(0)
            y_lo(0)
            for s in range(NSLOT):
                g, m = s // SLOTS, s % SLOTS
                b = g + 1
                if m == 0:
                    if b < NB:
                        topk_rounds(b, 0, 1)
                    if g >= 1:
                        tail_lo(g - 1)
                    route_first(g)
                    route_second(g)
                if 2 < m < 5 and b < NB:
                    topk_rounds(b, *TOPK_DONE[m:m + 2])
                if m == 7 and b < NB:
                    finish_x2(b)
                    if b + 1 < NB:
                        x_stats(b + 1)
                    normalise(b)
                if m == 8 and b < NB:
                    y_lo(b)
                hidden_up(s)
                hidden_c(s)
                if m == 0 and g >= 1:
                    add_moe(g - 1)
                if m == 1 and g >= 1:
                    add_shared(g - 1)
                if m <= 2 and b < NB:
                    topk_rounds(b, *TOPK_DONE[m:m + 2])
                if m == 5 and b < NB:
                    adjacency(b)
            tail_lo(NB - 1)
            add_moe(NB - 1)
            add_shared(NB - 1)

        @block.gpsimd
        def _(pool):
            def ln1_coefficients(b):
                v = ln1[:, b, :, :]
                n = 4 * b
                pool.wait_ge(mv1_done, 2 * (b + 1))
                pool.tensor_scalar(v[:, 0, :], mv1[:, b, :, 1], EPS, None, ALU.add).then_inc(ln1_step, 1)
                pool.wait_ge(ln1_step, n + 1)
                pool.tensor_tensor(v[:, 1, :], v[:, 0, :], half_col, ALU.pow).then_inc(ln1_step, 1)
                pool.wait_ge(ln1_step, n + 2)
                pool.tensor_scalar(v[:, 1, :], v[:, 1, :], c_res, None, ALU.mult).then_inc(ln1_step, 1)
                pool.wait_ge(ln1_step, n + 3)
                pool.tensor_scalar(v[:, 2, :], v[:, 1, :], 1.0, None, ALU.add)
                pool.tensor_tensor(v[:, 3, :], v[:, 1, :], mv1[:, b, :, 0], ALU.mult).then_inc(ln1_step, 1)
                pool.wait_ge(ln1_step, n + 4)
                pool.tensor_scalar(v[:, 3, :], v[:, 3, :], -1.0, None, ALU.mult).then_inc(ln1_done, 1)

            def rstd2(b):
                pool.wait_ge(mv2_done, 2 * (b + 1))
                pool.tensor_scalar(rs2[:, 0, :], mv2[:, :, 1], EPS, None, ALU.add).then_inc(rs2_step, 1)
                pool.wait_ge(rs2_step, b + 1)
                pool.tensor_tensor(rs2[:, 1, :], rs2[:, 0, :], half_col, ALU.pow).then_inc(rs2_done, 1)

            def weights_lo(n):
                w = min(PIECE, WCOLS - n * PIECE)
                cols = slice(n * PIECE, n * PIECE + w)
                pool.wait_ge(whi_done, n + 1)
                pool.tensor_tensor(w_lo[:, cols], raw[:, n % RING, 0:w], w_hi[:, cols].bitcast(F32),
                                   ALU.subtract).then_inc(wlo_done, 1)

            def hidden_lo(s):
                pool.wait_ge(hhi_done, s + 1)
                pool.tensor_tensor(h_lo[:, s % 3, :], h32[:, s % 2, :], h_hi[:, s % 3, :].bitcast(F32),
                                   ALU.subtract).then_inc(hlo_done, 1)

            half_col = minus_half.to_broadcast([P, 2])
            pool.dma_start(const_sb[:, :], const).then_inc(const_in, 16)
            pool.wait_ge(tscal_done, 2)
            pool.tensor_scalar(coef[:, 3:4], tscal[:, 2:3], 0.125, 0.125, ALU.mult, ALU.add).then_inc(coef_step, 1)
            pool.tensor_scalar(coef[:, 0:1], tscal[:, 2:3], -0.5, 0.5, ALU.mult, ALU.add).then_inc(coef_step, 1)
            pool.wait_ge(coef_step, 2)
            pool.tensor_tensor(coef[:, 2:3], coef[:, 3:4], tscal[:, 0:1], ALU.mult).then_inc(coef_step, 1)
            pool.tensor_tensor(coef[:, 1:2], coef[:, 0:1], tscal[:, 0:1], ALU.mult).then_inc(coef_step, 1)
            pool.wait_ge(coef_step, 4)
            ln1_coefficients(0)
            gw_in = gw_raw.rearrange("p (k e) -> p k e", k=KD)
            pool.tensor_copy(gw[:, :, 0:CW], gw_in).then_inc(gw_split, 1)
            pool.wait_ge(gw_split, 1)
            pool.tensor_tensor(gw[:, :, CW:2 * CW], gw_in, gw[:, :, 0:CW].bitcast(F32), ALU.subtract).then_inc(gw_split, 1)
            for n in range(EARLY):
                weights_lo(n)
                if n == EARLY - 2:
                    rstd2(0)
            ln1_coefficients(1)
            for s in range(NSLOT):
                g, m = s // SLOTS, s % SLOTS
                if m == 7 and g + 1 < NB:
                    rstd2(g + 1)
                if m < PAIRS:
                    hidden_lo(s)
                if g == 0 and EARLY + m < len(PIECES):
                    weights_lo(EARLY + m)
                if m == 1 and g >= 1 and g + 1 < NB:
                    ln1_coefficients(g + 1)


_SHAPE = (NB, NTOK, D)


def kernel(x, ctx_512, g_xattn, g_ffn, L0_xattn_Wq, L0_xattn_Wk, L0_xattn_gamma_raw, L0_ffn_gate_w, L0_ffn_w_gate,
           L0_ffn_w_up, L0_ffn_w_down, L0_ffn_sw_gate, L0_ffn_sw_up, L0_ffn_sw_down, L0_ffn_shared_gate_w):
    import numpy as np
    import concourse.bacc as bacc
    from concourse.bass_utils import run_bass_kernel_spmd

    f = np.float32
    a = np.asarray
    def side_by_side(shared, experts):
        return np.concatenate([shared[:, :SH_CH * P], experts, shared[:, SH_CH * P:]], axis=1)

    gate = side_by_side(a(L0_ffn_sw_gate), a(L0_ffn_w_gate).transpose(1, 0, 2).reshape(D, E * EI))
    up = side_by_side(a(L0_ffn_sw_up), a(L0_ffn_w_up).transpose(1, 0, 2).reshape(D, E * EI))
    down = side_by_side(a(L0_ffn_sw_down).T, a(L0_ffn_w_down).reshape(E * EI, D).T).T
    whole = CHUNKS * P
    gu = np.stack([gate[:, :whole], up[:, :whole]]).reshape(2, KD, P, CHUNKS, P).transpose(2, 3, 0, 1, 4)
    wd = down[:whole].reshape(CHUNKS, P, D).transpose(1, 0, 2)
    wpack = np.zeros((P, WCOLS), f)
    for n, (kind, c) in enumerate(PIECES):
        at = n * PIECE
        if kind == "gu":
            wpack[:, at:at + PIECE] = gu[:, c:c + 2].reshape(P, PIECE)
        elif kind == "wd":
            wpack[:, at:at + PIECE] = wd[:, c:c + 4].reshape(P, PIECE)
        else:
            both = np.concatenate([gate[:, whole:], up[:, whole:]], axis=1)
            wpack[:, at:at + 256] = both.reshape(KD, P, P).transpose(1, 0, 2).reshape(P, KD * P)
            wpack[:, at + 256:at + 512] = np.tile(down[whole:], (2, 1))
    const = np.zeros((P, CONST), f)
    const[:, 0:P] = np.eye(P, dtype=f)
    const[:, C_IOTA:C_IOTA + 8] = np.arange(8, dtype=f)
    const[:, C_HALF] = -0.5
    for n, v in enumerate((g_xattn, g_ffn, L0_xattn_gamma_raw)):
        const[:, C_SCAL + n] = a(v).reshape(-1)[0]
    gw = const[:, C_GW:].reshape(P, KD, CW)
    gw[:, :, 0:E] = a(L0_ffn_gate_w).T.reshape(KD, P, E).transpose(1, 0, 2)
    gw[:, :, E] = a(L0_ffn_shared_gate_w).reshape(KD, P).T
    const[:, C_GW:] = gw.reshape(P, KD * CW)
    arrays = {
        "x": np.ascontiguousarray(x),
        "qk_in": np.concatenate([a(L0_xattn_Wq).T, a(L0_xattn_Wk).T,
                                 a(ctx_512).transpose(2, 0, 1).reshape(DC, NB * NTOK)], axis=1),
        "const": const,
        "wpack": wpack,
    }
    nc = bacc.Bacc("TRN2", target_bir_lowering=False, num_devices=1)
    aps = [nc.dram_tensor(n, v.shape, mybir.dt.from_np(v.dtype), kind="ExternalInput").ap() for n, v in arrays.items()]
    out = nc.dram_tensor("out", _SHAPE, F32, kind="ExternalOutput").ap()
    build(nc, *aps, out)
    r = run_bass_kernel_spmd(nc, [arrays], core_ids=[0])
    return r.results[0]["out"]
```
